# Optimizing a Trainium2 kernel written in Bass

```python
import numpy as np
import jax
import jax.numpy as jnp

def _softmax(x, axis=-1):
    return jax.nn.softmax(x, axis=axis)

def _gelu(x):
    return jax.nn.gelu(x, approximate=True)

def _silu(x):
    return jax.nn.silu(x)

def _sigmoid(x):
    return jax.nn.sigmoid(x)

def _layernorm(x, axis=-1, eps=1e-05):
    m = jnp.mean(x, axis=axis, keepdims=True)
    v = jnp.var(x, axis=axis, keepdims=True)
    return (x - m) / jnp.sqrt(v + eps)

def _scatter_add(tgt, idx, src, axis=0):
    return tgt.at[idx].add(src)

def _segment_sum(src, seg, n):
    return jax.ops.segment_sum(src, seg, n)
kernel_name = 'mk_adj_preln_d2_adj_r2_9d97a6'

def setup_inputs(seed: int=0):
    np.random.seed(seed)
    _w = jnp.asarray

    def _rec_inputs():
        import jax
        import jax.numpy as jnp
        _gk = jax.random.key(seed)
        x = -0.0002928 + 1 * jax.random.normal(jax.random.fold_in(_gk, 1), (8192, 128), jnp.float32)
        _a = jax.random.bernoulli(jax.random.fold_in(_gk, 2), 0.00195312, (8192, 8192))
        _a = jnp.logical_or(_a, jnp.swapaxes(_a, -1, -2))
        _a = jnp.logical_or(_a, jnp.eye(8192, dtype=bool))
        adj = _a.astype(jnp.int32)
        return (x, adj)
    x, adj = _rec_inputs()

    def _L0_gnn_setup():
        import jax, jax.numpy as jnp
        import numpy as np
        N = 8192
        D = 128
        key = jax.random.key(seed)
        k1, k2, k3, k4 = jax.random.split(key, 4)
        x = jax.random.normal(k1, (N, D), dtype=jnp.float32)
        adj = jax.random.randint(k2, (N, N), 0, 2, dtype=jnp.int32)
        W = jax.random.normal(k3, (D, D), dtype=jnp.float32) * 0.05
        b = jax.random.normal(k4, (D,), dtype=jnp.float32) * 0.05
        return {'x': x, 'adj': adj, 'W': W, 'b': b}
    _L0_gnn_all = _L0_gnn_setup()
    _L0_gnn_in = {k: v for k, v in _L0_gnn_all.items() if k in ('W', 'b')}
    del _L0_gnn_all

    def _L1_gnn_setup():
        import jax, jax.numpy as jnp
        import numpy as np
        N = 4096
        F_IN = 128
        F_OUT = 128
        ALPHA = 0.2
        NEG_BIG = -9000000000000000.0
        key = jax.random.key(seed)
        k1, k2, k3, k4 = jax.random.split(key, 4)
        h = jax.random.normal(k1, (N, F_IN), dtype=jnp.float32)
        adj = jax.random.randint(k2, (N, N), 0, 2, dtype=jnp.int32)
        W = jax.random.normal(k3, (F_IN, F_OUT), dtype=jnp.float32) * (1.414 / np.sqrt(F_IN))
        a = jax.random.normal(k4, (2 * F_OUT, 1), dtype=jnp.float32) * (1.414 / np.sqrt(2 * F_OUT))
        return {'h': h, 'adj': adj, 'W': W, 'a': a}
    _L1_gnn_all = _L1_gnn_setup()
    _L1_gnn_in = {k: v for k, v in _L1_gnn_all.items() if k in ('W', 'a')}
    del _L1_gnn_all
    return {'x': x, 'adj': adj, 'L0_gnn_W': _L0_gnn_in['W'], 'L0_gnn_b': _L0_gnn_in['b'], 'L1_gnn_W': _L1_gnn_in['W'], 'L1_gnn_a': _L1_gnn_in['a']}

def reference(x, adj, L0_gnn_W, L0_gnn_b, L1_gnn_W, L1_gnn_a):
    import jax
    import jax.numpy as jnp

    def _L0_gnn_ref(x, adj, W, b):
        import jax, jax.numpy as jnp
        import numpy as np
        N = 8192
        D = 128
        a = (adj == 1).astype(x.dtype)
        deg = jnp.sum(a, axis=1, keepdims=True)
        agg = jnp.einsum('ij,jf->if', a, x) / deg
        return agg @ W.T + b

    def _L1_gnn_ref(h, adj, W, a):
        import jax, jax.numpy as jnp
        import numpy as np
        N = 4096
        F_IN = 128
        F_OUT = 128
        ALPHA = 0.2
        NEG_BIG = -9000000000000000.0
        wh = h @ W
        wh1 = wh @ a[:F_OUT, :]
        wh2 = wh @ a[F_OUT:, :]
        e = wh1 + wh2.T
        e = jnp.where(e > 0, e, ALPHA * e)
        e = jnp.where(adj > 0, e, NEG_BIG)
        attention = jax.nn.softmax(e, axis=-1)
        h_prime = attention @ wh
        return jax.nn.elu(h_prime)
    h = jnp.maximum(_layernorm(x, axis=-1), 0.0)
    x = x + _L0_gnn_ref(h, adj, L0_gnn_W, L0_gnn_b)
    h = jnp.maximum(_layernorm(x, axis=-1), 0.0)
    x = x + _L1_gnn_ref(h, adj, L1_gnn_W, L1_gnn_a)
    return x

_drawn_inputs = setup_inputs


def setup_inputs(seed=0):
    import zlib

    import numpy as np

    out = dict(_drawn_inputs(seed))
    spreads = {}
    factors = {}
    for name, (base, spread) in spreads.items():
        noise = np.random.default_rng([zlib.crc32(name.encode()), seed]).standard_normal(out[name].shape)
        drawn = base * np.exp(spread * noise) if base else spread * noise
        out[name] = jnp.asarray(drawn.astype(out[name].dtype))
    for name, factor in factors.items():
        out[name] = (out[name] * factor).astype(out[name].dtype)
    return out
```

```python
from contextlib import ExitStack

import concourse.bass as bass
from concourse import mybir

P = 128
LEAK = 0.2
LN_EPS = 1e-5
LIFT = 36.0
LO_SCALE = 2048.0
GATE = 64.0

ALU = mybir.AluOpType
ACT = mybir.ActivationFunctionType
F32 = mybir.dt.float32
F16 = mybir.dt.float16
BF16 = mybir.dt.bfloat16
U8 = mybir.dt.uint8
I32 = mybir.dt.int32


def two_layer_gnn(nc, x, adj, w0t, b0, w1, a, out):
    D = x.shape[2]
    BLOCKS = adj.shape[0]
    CHUNKS = adj.shape[1]
    TJ = adj.shape[3]
    BLK = adj.shape[4]
    JT = CHUNKS * TJ
    QUARTERS = 4
    QC = CHUNKS // QUARTERS
    ADJ_RING = 6
    EQ_RING = 2 * QC
    GT_RING = QC
    SEG = 4
    HW = 2 * D + 1
    YW = D + 1
    NQ = BLOCKS * QUARTERS
    assert TJ * P == BLK and BLOCKS * TJ == JT and QC == 4 and BLOCKS == CHUNKS

    strips, segments, segment_at = [], [], {}

    def add_segment(lo, hi, when):
        if hi > lo:
            segment_at.setdefault(when, []).append(len(segments))
            segments.append((len(strips), lo, hi))

    for s in range(BLOCKS - 1):
        for q in range(QUARTERS):
            add_segment((s + 1) * q // QUARTERS, (s + 1) * (q + 1) // QUARTERS, (s + 2, q))
        strips.append((s, 0, s + 1))
    for s in range(BLOCKS - 1, -1, -1):
        first = s + 1 if s < BLOCKS - 1 else 0
        for lo in range(first, BLOCKS, SEG):
            add_segment(lo, min(lo + SEG, BLOCKS), ("upper", s))
        strips.append((s, first, BLOCKS))
    LOWER = BLOCKS - 1
    strip_last_segment = {m: z for z, (m, _, _) in enumerate(segments)}
    units_before, n = [], 0
    for _, lo, hi in segments:
        units_before.append(n)
        n += TJ * (hi - lo)
    units_upto_strip = {m: units_before[z] + TJ * (segments[z][2] - segments[z][1])
                        for m, z in strip_last_segment.items()}

    def strip_of_upper(s):
        return LOWER + BLOCKS - 1 - s

    gt_dram = nc.dram_tensor("gt_masks", [BLOCKS, P, JT, BLK], U8, kind="Internal").ap()
    r_dram = nc.dram_tensor("r_rows", [BLOCKS, P, BLK], F32, kind="Internal").ap()
    x1_dram = nc.dram_tensor("x1_rows", [BLOCKS, P, TJ, D], F32, kind="Internal").ap()
    low_dram = nc.dram_tensor("lower_sums", [BLOCKS, P, TJ, YW], F32, kind="Internal").ap()

    ctx = ExitStack()
    with ctx:
        def sb(name, shape, dt):
            return ctx.enter_context(nc.sbuf_tensor(name, shape, dt))

        def ps(name, shape):
            return ctx.enter_context(nc.psum_tensor(name, shape, F32))

        def sem(name):
            return ctx.enter_context(nc.semaphore(name))

        h = sb("h", [P, JT, HW], F16)
        y = sb("y", [P, JT, YW], F32)
        adj_in = sb("adj_in", [P, ADJ_RING, TJ, BLK], I32)
        eq = sb("eq", [P, EQ_RING, TJ, BLK], BF16)
        gt = sb("gt", [P, GT_RING, TJ, BLK], U8)
        strip_mask = sb("strip_mask", [P, 2, SEG * TJ, BLK], U8)
        prob = sb("prob", [P, TJ, BLK], F32)
        r_row = sb("r_row", [P, 2, BLK], F32)
        strip_sum = sb("strip_sum", [P, 2, TJ, YW], F32)
        low_in = sb("low_in", [P, 2, TJ, YW], F32)
        xb = sb("xb", [P, TJ, D], F32)
        x1 = sb("x1", [P, 2, TJ, D], F32)
        agg_raw = low_in[:].rearrange("p r t f -> p (r t f)")[:, 0:TJ * HW].rearrange("p (t f) -> p t f", t=TJ)
        agg = sb("agg", [P, TJ, D], F32)
        feat_t = sb("feat_t", [P, TJ, P], F32)
        stats = sb("stats", [P, JT, 6], F32)
        mean_var = sb("mean_var", [P, JT, 2], F32)
        rstd = sb("rstd", [P, JT], F32)
        rdeg = sb("rdeg", [P, TJ], F32)
        g_col = sb("g_col", [P, JT], F32)
        v_col = sb("v_col", [P, TJ], F32)
        fin_rec = sb("fin_rec", [P, TJ], F32)
        ident = sb("ident", [P, P], F32)
        w0t_s = sb("w0t_s", [P, D], F32)
        w1_s = sb("w1_s", [P, D], F32)
        b_s = sb("b_s", [P, D], F32)
        a_s = sb("a_s", [P, 2, D], F32)
        wa = sb("wa", [P, 2], F32)
        wa_rep = sb("wa_rep", [P, 2, P], F32)
        junk = sb("junk", [P, TJ, D], F32)
        ones = sb("ones", [P, P], F32)
        vmax = sb("vmax", [P, 1], F32)
        cst = sb("cst", [P, 5], F32)
        g_bias, f_bias, r_bias = cst[:, 0:1], cst[:, 1:2], cst[:, 2:3]
        gate_bias, eps = cst[:, 3:4], cst[:, 4:5]
        neg = feat_t
        pos = agg

        bank = 512
        agg_ps = ps("agg_ps", [P, TJ, bank])
        strip_ps = ps("strip_ps", [P, 2, bank])
        turn_ps = ps("turn_ps", [P, bank])
        proj_ps = ps("proj_ps", [P, bank])

        def strip_out(i):
            return strip_ps[:, i // 2, (i % 2) * YW:(i % 2 + 1) * YW]

        const_loaded = sem("const_loaded")
        x_loaded = [sem(f"x_loaded{q}") for q in range(QUARTERS)]
        adj_loaded = [sem(f"adj_loaded{r}") for r in range(ADJ_RING)]
        gt_stored = [sem(f"gt_stored{r}") for r in range(GT_RING)]
        mask_loaded = [sem(f"mask_loaded{r}") for r in range(2)]
        xblk_loaded = sem("xblk_loaded")
        rows_stored = [sem(f"rows_stored{r}") for r in range(2)]
        sums_stored = [sem(f"sums_stored{r}") for r in range(2)]
        r_loaded = [sem(f"r_loaded{r}") for r in range(2)]
        rest_loaded = [sem(f"rest_loaded{r}") for r in range(2)]
        out_stored = sem("out_stored")
        ident_zero = sem("ident_zero")
        ident_made = sem("ident_made")
        xb_made = sem("xb_made")
        cst_made = sem("cst_made")
        ln_stat = sem("ln_stat")
        ln_std = sem("ln_std")
        ln_low = sem("ln_low")
        h_made = sem("h_made")
        wa_made = sem("wa_made")
        norm_made = sem("norm_made")
        norm_taken = sem("norm_taken")
        vmax_made = sem("vmax_made")
        dve_step = sem("dve_step")
        eq_made = sem("eq_made")
        gt_made = sem("gt_made")
        eq_used = sem("eq_used")
        agg_taken = sem("agg_taken")
        agg_made = sem("agg_made")
        turn_done = sem("turn_done")
        turn_taken = sem("turn_taken")
        proj_done = sem("proj_done")
        x1_made = sem("x1_made")
        dev_ready = sem("dev_ready")
        std_made = sem("std_made")
        h1_made = sem("h1_made")
        v_made = sem("v_made")
        gf_made = sem("gf_made")
        u_made = sem("u_made")
        y_made = sem("y_made")
        r_made = sem("r_made")
        prob_made = sem("prob_made")
        prob_used = sem("prob_used")
        strip_taken = sem("strip_taken")
        neg_made = sem("neg_made")
        exp_made = sem("exp_made")
        out_made = sem("out_made")

        block = ctx.enter_context(nc.Block())

        @block.sync
        def _(sp):
            def load_adj(g):
                if g >= ADJ_RING:
                    sp.wait_ge(eq_made, g - ADJ_RING + 1)
                    sp.wait_ge(gt_made, g - ADJ_RING + 1)
                sp.dma_start(adj_in[:, g % ADJ_RING], adj[g // CHUNKS, g % CHUNKS])\
                  .then_inc(adj_loaded[g % ADJ_RING], 16)

            def store_gt(g):
                t, c = divmod(g, CHUNKS)
                sp.wait_ge(gt_made, g + 1)
                sp.dma_start(gt_dram[t, :, c * TJ:(c + 1) * TJ, :], gt[:, g % GT_RING])\
                  .then_inc(gt_stored[g % GT_RING], 16)

            def load_mask(z):
                m, lo, hi = segments[z]
                s = strips[m][0]
                for r in range(GT_RING):
                    sp.wait_ge(gt_stored[r], 16 * (s + 1) * CHUNKS // GT_RING)
                if z >= 2:
                    sp.wait_ge(prob_made, units_before[z - 1])
                sp.dma_start(strip_mask[:, z % 2, 0:TJ * (hi - lo), :],
                             gt_dram[s, :, TJ * lo:TJ * hi, :]).then_inc(mask_loaded[z % 2], 16)

            def load_x_block(t):
                if t >= 1:
                    sp.wait_ge(x1_made, t)
                sp.dma_start(xb[:], x[t * TJ:(t + 1) * TJ].rearrange("t p d -> p t d")).then_inc(xblk_loaded, 16)

            def store_rows(t):
                sp.wait_ge(x1_made, t + 1)
                sp.dma_start(x1_dram[t], x1[:, t % 2]).then_inc(rows_stored[t % 2], 16)
                sp.wait_ge(r_made, t + 1)
                sp.dma_start(r_dram[t], r_row[:, t % 2, :]).then_inc(rows_stored[t % 2], 16)

            def store_sums(s):
                sp.wait_ge(strip_taken, s + 1)
                sp.dma_start(low_dram[s], strip_sum[:, s % 2]).then_inc(sums_stored[s % 2], 16)

            def load_r(s):
                if s > BLOCKS - 3:
                    return
                for r in range(2):
                    sp.wait_ge(rows_stored[r], 32 * BLOCKS // 2)
                sp.wait_ge(prob_made, units_upto_strip[strip_of_upper(s + 2)])
                sp.dma_start(r_row[:, s % 2, :], r_dram[s]).then_inc(r_loaded[s % 2], 16)

            def load_rest(s):
                if s <= BLOCKS - 3:
                    sp.wait_ge(out_made, BLOCKS - 2 - s)
                    sp.dma_start(x1[:, s % 2], x1_dram[s]).then_inc(rest_loaded[s % 2], 16)
                if s < BLOCKS - 1:
                    for r in range(2):
                        sp.wait_ge(sums_stored[r], 16 * ((LOWER + 1 - r) // 2))
                    sp.dma_start(low_in[:, s % 2], low_dram[s]).then_inc(rest_loaded[s % 2], 16)

            def store_out(s):
                sp.wait_ge(out_made, BLOCKS - s)
                sp.dma_start(out[s * TJ:(s + 1) * TJ].rearrange("t p d -> p t d"), pos[:]).then_inc(out_stored, 16)

            for g in range(ADJ_RING):
                load_adj(g)
            for t in range(BLOCKS + 1):
                for q in range(QUARTERS):
                    Q = t * QUARTERS + q
                    if t < BLOCKS:
                        for g in range(Q * QC, (Q + 1) * QC):
                            store_gt(g)
                            if g + ADJ_RING < BLOCKS * CHUNKS:
                                load_adj(g + ADJ_RING)
                    nt, nq = divmod(Q + 1, QUARTERS)
                    for z in segment_at.get((nt, nq), []):
                        load_mask(z)
                    if q == 3 and t < BLOCKS:
                        load_x_block(t)
                    if q == 0 and t >= 2:
                        store_rows(t - 2)
                    if q == 1 and t >= 3:
                        store_sums(t - 3)
            for s in range(BLOCKS - 1, -1, -1):
                load_r(s)
                for z in segment_at.get(("upper", s), []):
                    load_mask(z)
                if s == BLOCKS - 1:
                    store_rows(BLOCKS - 1)
                    store_sums(LOWER - 1)
                load_rest(s)
                if s + 2 < BLOCKS:
                    store_out(s + 2)
            store_out(1)
            store_out(0)
            sp.wait_ge(out_stored, 16 * BLOCKS)

        @block.gpsimd
        def _(pool):
            nc.gpsimd.memset(ident[:], 0.0).then_inc(ident_zero, 1)
            nc.gpsimd.memset(ones[:], 1.0).then_inc(ident_zero, 1)
            nc.gpsimd.memset(h[:, :, 2 * D:HW], 1.0).then_inc(ident_zero, 1)
            nc.gpsimd.memset(cst[:, 2:3], LIFT).then_inc(ident_zero, 1)
            nc.gpsimd.memset(cst[:, 3:4], -GATE / 2).then_inc(ident_zero, 1)
            nc.gpsimd.memset(cst[:, 4:5], LN_EPS).then_inc(ident_zero, 1)
            pool.wait_ge(ident_zero, 6)
            nc.gpsimd.affine_select(out=ident[:], in_=ident[:], compare_op=ALU.not_equal, fill=1.0, base=0,
                                    pattern=[[-1, P]], channel_multiplier=1).then_inc(ident_made, 1)
            pool.wait_ge(const_loaded, 16 * 5)
            for t in range(BLOCKS):
                pool.wait_ge(xblk_loaded, 16 * (t + 1))
                for i in range(TJ):
                    last = nc.gpsimd.tensor_tensor(xb[:, i, :], xb[:, i, :], b_s[:], ALU.add)
                last.then_inc(xb_made, 1)

        @block.scalar
        def _(act):
            for q in range(QUARTERS):
                n = JT // QUARTERS
                act.dma_start(y[:, q * n:(q + 1) * n, 0:D],
                              x[q * n:(q + 1) * n].rearrange("t p d -> p t d")).then_inc(x_loaded[q], 16)
            act.dma_start(w1_s[:], w1).then_inc(const_loaded, 16)
            act.dma_start(w0t_s[:], w0t).then_inc(const_loaded, 16)
            act.dma_start(b_s[:], b0.partition_broadcast(P)).then_inc(const_loaded, 16)
            act.dma_start(a_s[:, 0, :], a[0].partition_broadcast(P)).then_inc(const_loaded, 16)
            act.dma_start(a_s[:, 1, :], a[1].partition_broadcast(P)).then_inc(const_loaded, 16)
            act.wait_ge(ident_made, 1)

            def gates(Q):
                for g in range(Q * QC, (Q + 1) * QC):
                    act.wait_ge(adj_loaded[g % ADJ_RING], 16 * (g // ADJ_RING + 1))
                    if g >= GT_RING:
                        act.wait_ge(gt_stored[g % GT_RING], 16 * (g // GT_RING))
                    nc.scalar.activation(gt[:, g % GT_RING], adj_in[:, g % ADJ_RING], ACT.Sigmoid,
                                         bias=gate_bias, scale=GATE).then_inc(gt_made, 1)

            def split_h(q):
                n = JT // QUARTERS
                j = slice(q * n, (q + 1) * n)
                act.wait_ge(ln_stat, q + 1)
                nc.scalar.activation(rstd[:, j], mean_var[:, j, 1], ACT.Sqrt, bias=eps).then_inc(ln_std, 1)
                act.wait_ge(ln_low, q + 1)
                nc.scalar.activation(h[:, j, D:2 * D], y[:, j, 0:D], ACT.Copy, scale=LO_SCALE).then_inc(h_made, 1)

            def take_strip(m):
                act.wait_ge(prob_used, units_upto_strip[m])
                if 2 <= m < LOWER + 2:
                    act.wait_ge(sums_stored[m % 2], 16 * (m // 2))
                if m >= LOWER + 2:
                    act.wait_ge(out_made, m - LOWER - 1)
                for b in range(2):
                    last = nc.scalar.activation(strip_sum[:, m % 2, 2 * b:2 * b + 2, :],
                                                strip_ps[:, b, 0:2 * YW].rearrange("p (t f) -> p t f", t=2),
                                                ACT.Copy)
                last.then_inc(strip_taken, 1)

            def take_turn(n):
                t, second = divmod(n, 2)
                act.wait_ge(turn_done, 3 * t + second + 1)
                if second == 0 and t >= 1:
                    act.wait_ge(turn_done, 3 * t)
                if second == 1:
                    act.wait_ge(proj_done, 2 * t + 1)
                nc.scalar.activation(feat_t[:].rearrange("p t f -> p (t f)"), turn_ps[:],
                                     ACT.Copy).then_inc(turn_taken, 1)

            split_h(0)
            gates(0)
            for t in range(BLOCKS + 1):
                e = t - 1
                for q in range(QUARTERS):
                    if t == 0 and q + 1 < QUARTERS:
                        split_h(q + 1)
                    if t * QUARTERS + q + 1 < NQ:
                        gates(t * QUARTERS + q + 1)
                    if q == 0:
                        if 0 <= t - 3:
                            take_strip(t - 3)
                        if e >= 0:
                            take_turn(2 * e)
                    if q == 3 and t == 0:
                        act.wait_ge(norm_made, 1)
                        nc.scalar.activation(vmax[:], turn_ps[:, 0:1], ACT.Sqrt, scale=float(D))\
                          .then_inc(norm_taken, 1)
                    if q == 1 and e >= 0:
                        act.wait_ge(dev_ready, e + 1)
                        nc.scalar.activation(rstd[:, 0:TJ], mean_var[:, 0:TJ, 1], ACT.Sqrt,
                                             bias=eps).then_inc(std_made, 1)
                    if q == 2 and e >= 0:
                        take_turn(2 * e + 1)
                    if q == 3 and e >= 0:
                        if e == 0:
                            act.wait_ge(vmax_made, 2)
                        js = slice(e * TJ, (e + 1) * TJ)
                        act.wait_ge(v_made, e + 1)
                        nc.scalar.activation(g_col[:, js], v_col[:], ACT.Exp, bias=g_bias, scale=1.0 - LEAK)
                        nc.scalar.activation(y[:, js, D], v_col[:], ACT.Exp, bias=f_bias,
                                             scale=LEAK).then_inc(gf_made, 1)
                        act.wait_ge(u_made, e + 1)
                        nc.scalar.activation(r_row[:, e % 2, :], r_row[:, e % 2, :], ACT.Exp, bias=r_bias,
                                             scale=LEAK - 1.0).then_inc(r_made, 1)
                        act.wait_ge(gf_made, e + 1)
                        for i in range(TJ):
                            last = nc.scalar.activation(y[:, e * TJ + i, 0:D], proj_ps[:, i * D:(i + 1) * D],
                                                        ACT.Copy, scale=y[:, e * TJ + i, D:YW])
                        last.then_inc(y_made, 1)
                    if q == 3 and t < BLOCKS:
                        act.wait_ge(eq_used, CHUNKS * (t + 1))
                        if t >= 1:
                            act.wait_ge(agg_made, t)
                        nc.scalar.activation(agg_raw, agg_ps[:, :, 0:HW], ACT.Copy).then_inc(agg_taken, 1)
            take_strip(LOWER - 1)
            for s in range(BLOCKS - 1, -1, -1):
                if s < BLOCKS - 1:
                    act.wait_ge(neg_made, BLOCKS - 1 - s)
                    nc.scalar.activation(neg[:], neg[:], ACT.Exp).then_inc(exp_made, 1)
                take_strip(strip_of_upper(s))
            act.wait_ge(neg_made, BLOCKS)
            nc.scalar.activation(neg[:], neg[:], ACT.Exp).then_inc(exp_made, 1)

        @block.vector
        def _(dve):
            links = [0]

            def link(instruction):
                links[0] += 1
                instruction.then_inc(dve_step, 1)
                dve.wait_ge(dve_step, links[0])

            def layer_norm_x(q):
                n = JT // QUARTERS
                js = slice(q * n, (q + 1) * n)
                dve.wait_ge(x_loaded[q], 16)
                for j in range(q * n, (q + 1) * n):
                    last = nc.vector.bn_stats(stats[:, j, :], y[:, j, 0:D])
                link(last)
                for j in range(q * n, (q + 1) * n):
                    last = nc.vector.bn_aggr(mean_var[:, j, :], stats[:, j, :])
                last.then_inc(ln_stat, 1)
                dve.wait_ge(ln_stat, q + 1)
                dve.wait_ge(ln_std, q + 1)
                link(nc.vector.reciprocal(rstd[:, js], rstd[:, js]))
                for j in range(q * n, (q + 1) * n):
                    last = nc.vector.tensor_scalar(y[:, j, 0:D], y[:, j, 0:D], mean_var[:, j, 0:1],
                                                   rstd[:, j:j + 1], ALU.subtract, ALU.mult)
                link(last)
                link(nc.vector.tensor_scalar(h[:, js, 0:D], y[:, js, 0:D], 0.0, None, ALU.max))
                nc.vector.scalar_tensor_tensor(out=y[:, js, 0:D], in0=y[:, js, 0:D], scalar=0.0,
                                               in1=h[:, js, 0:D], op0=ALU.max, op1=ALU.subtract)\
                    .then_inc(ln_low, 1)

            def equals(Q):
                for g in range(Q * QC, (Q + 1) * QC):
                    dve.wait_ge(adj_loaded[g % ADJ_RING], 16 * (g // ADJ_RING + 1))
                    if g >= EQ_RING:
                        dve.wait_ge(eq_used, g - EQ_RING + 1)
                    nc.vector.tensor_scalar(eq[:, g % EQ_RING], adj_in[:, g % ADJ_RING], 1.0, None,
                                            ALU.is_equal).then_inc(eq_made, 1)

            def weights(z):
                m, lo, hi = segments[z]
                s = strips[m][0]
                if lo == strips[m][1]:
                    if m < LOWER or s == BLOCKS - 1:
                        dve.wait_ge(r_made, s + 1)
                    if m > LOWER and s <= BLOCKS - 3:
                        dve.wait_ge(r_loaded[s % 2], 16 * ((BLOCKS - 1 - s) // 2))
                dve.wait_ge(mask_loaded[z % 2], 16 * (z // 2 + 1))

                def column_block(b):
                    for k in range(TJ):
                        if units_before[z] > 0:
                            dve.wait_ge(prob_used, b * TJ + (units_before[z] + k - TJ + 1))
                        nc.vector.scalar_tensor_tensor(
                            out=prob[:, k, :], in0=r_row[:, s % 2, :],
                            scalar=g_col[:, bass.ds(b * TJ + (lo * TJ + k), 1)],
                            in1=strip_mask[:, z % 2, bass.ds(b * TJ + k, 1), :].rearrange("p o f -> p (o f)"),
                            op0=ALU.max, op1=ALU.mult).then_inc(prob_made, 1)

                if hi - lo == 1:
                    column_block(0)
                else:
                    assert units_before[z] > 0
                    with dve.Fori(0, hi - lo) as b:
                        column_block(b)

            def sum_halves(e):
                dve.wait_ge(agg_taken, e + 1)
                if e >= 1:
                    dve.wait_ge(turn_done, 3 * e - 1)
                nc.vector.reciprocal(rdeg[:], agg_raw[:, :, 2 * D])
                nc.vector.scalar_tensor_tensor(out=agg[:], in0=agg_raw[:, :, D:2 * D], scalar=1.0 / LO_SCALE,
                                               in1=agg_raw[:, :, 0:D], op0=ALU.mult,
                                               op1=ALU.add).then_inc(agg_made, 1)

            def residual_norm(e):
                dve.wait_ge(agg_made, e + 1)
                dve.wait_ge(proj_done, 2 * e + 1)
                dve.wait_ge(xb_made, e + 1)
                if e >= 2:
                    dve.wait_ge(rows_stored[e % 2], 32 * (e // 2))
                for i in range(TJ):
                    last = nc.vector.scalar_tensor_tensor(out=x1[:, e % 2, i, :], in0=proj_ps[:, i * D:(i + 1) * D],
                                                          scalar=rdeg[:, i:i + 1], in1=xb[:, i, :],
                                                          op0=ALU.mult, op1=ALU.add)
                last.then_inc(x1_made, 1)
                dve.wait_ge(x1_made, e + 1)
                for i in range(TJ):
                    last = nc.vector.bn_stats(stats[:, i, :], x1[:, e % 2, i, :])
                link(last)
                for i in range(TJ):
                    last = nc.vector.bn_aggr(mean_var[:, i, :], stats[:, i, :])
                last.then_inc(dev_ready, 1)
                dve.wait_ge(dev_ready, e + 1)
                dve.wait_ge(std_made, e + 1)
                link(nc.vector.reciprocal(rstd[:, 0:TJ], rstd[:, 0:TJ]))
                for i in range(TJ):
                    last = nc.vector.tensor_scalar(agg[:, i, :], x1[:, e % 2, i, :], mean_var[:, i, 0:1],
                                                   rstd[:, i:i + 1], ALU.subtract, ALU.mult)
                link(last)
                nc.vector.tensor_scalar(agg[:], agg[:], 0.0, None, ALU.max).then_inc(h1_made, 1)

            def logits(e):
                dve.wait_ge(proj_done, 2 * e + 2)
                if e >= 1:
                    dve.wait_ge(gf_made, e)
                for i in range(TJ):
                    last = nc.vector.tensor_tensor_reduce(junk[:, i, :], proj_ps[:, i * D:(i + 1) * D], a_s[:, 1, :],
                                                          1.0, 0.0, ALU.mult, ALU.add, v_col[:, i:i + 1])
                last.then_inc(v_made, 1)
                dve.wait_ge(turn_done, 3 * e + 3)
                if e >= 2:
                    dve.wait_ge(rows_stored[e % 2], 32 * (e // 2))
                nc.vector.tensor_scalar(r_row[:, e % 2, :], turn_ps[:], vmax[:, 0:1], 0.0,
                                        ALU.add, ALU.max).then_inc(u_made, 1)

            def finish(s):
                m = strip_of_upper(s)
                slot = s % 2
                dve.wait_ge(strip_taken, m + 1)
                if s < BLOCKS - 1:
                    dve.wait_ge(rest_loaded[slot], 32 * ((BLOCKS - 1 - s) // 2) + (16 if s % 2 == BLOCKS % 2 else 0))
                total = strip_sum[:, m % 2]
                if s < BLOCKS - 1:
                    link(nc.vector.tensor_tensor(total, total, low_in[:, slot], ALU.add))
                link(nc.vector.reciprocal(fin_rec[:], total[:, :, D]))
                if s < BLOCKS - 1:
                    dve.wait_ge(out_stored, 16 * (BLOCKS - 1 - s))
                for i in range(TJ):
                    last = nc.vector.tensor_scalar(neg[:, i, :], total[:, i, 0:D], fin_rec[:, i:i + 1], 0.0,
                                                   ALU.mult, ALU.min)
                last.then_inc(neg_made, 1)
                for i in range(TJ):
                    last = nc.vector.tensor_scalar(pos[:, i, :], total[:, i, 0:D], fin_rec[:, i:i + 1], 0.0,
                                                   ALU.mult, ALU.max)
                link(last)
                link(nc.vector.tensor_tensor(pos[:], pos[:], x1[:, slot], ALU.add))
                dve.wait_ge(exp_made, BLOCKS - s)
                nc.vector.scalar_tensor_tensor(out=pos[:], in0=neg[:], scalar=-1.0, in1=pos[:],
                                               op0=ALU.add, op1=ALU.add).then_inc(out_made, 1)

            dve.wait_ge(ident_made, 1)
            layer_norm_x(0)
            equals(0)
            for t in range(BLOCKS + 1):
                e = t - 1
                for q in range(QUARTERS):
                    if t == 0 and q + 1 < QUARTERS:
                        layer_norm_x(q + 1)
                    if t * QUARTERS + q + 1 < NQ:
                        equals(t * QUARTERS + q + 1)
                    if t == 0 and q == 3:
                        dve.wait_ge(const_loaded, 16 * 5)
                        for k in range(2):
                            link(nc.vector.tensor_tensor_reduce(junk[:, k, :], w1_s[:], a_s[:, k, :], 1.0, 0.0, ALU.mult,
                                                                ALU.add, wa[:, k:k + 1]))
                            last = nc.vector.tensor_scalar(wa_rep[:, k, :], ones[:], wa[:, k:k + 1], None, ALU.mult)
                        last.then_inc(wa_made, 1)
                        dve.wait_ge(norm_taken, 1)
                        nc.vector.tensor_scalar(cst[:, 0:1], vmax[:], LEAK - 1.0, LIFT, ALU.mult,
                                                ALU.add).then_inc(vmax_made, 1)
                        nc.vector.tensor_scalar(cst[:, 1:2], vmax[:], -LEAK, LIFT, ALU.mult,
                                                ALU.add).then_inc(vmax_made, 1)
                    if e >= 0:
                        if q == 0:
                            sum_halves(e)
                        if q == 1:
                            residual_norm(e)
                        if q == 3:
                            logits(e)
                    for z in segment_at.get((t, q), []):
                        weights(z)
            for s in range(BLOCKS - 1, -1, -1):
                for z in segment_at.get(("upper", s), []):
                    weights(z)
                if s < BLOCKS - 1:
                    finish(s + 1)
            finish(0)

        @block.tensor
        def _(pe):
            def aggregate(Q):
                t, q = divmod(Q, QUARTERS)
                if t == 0:
                    pe.wait_ge(h_made, q + 1)
                if q == 0 and t >= 1:
                    pe.wait_ge(agg_taken, t)

                def chunk(c, first=False, last=False):
                    pe.wait_ge(eq_made, c + (Q * QC + 1))
                    for k in range(TJ):
                        for i in range(TJ):
                            mm = nc.tensor.matmul(
                                agg_ps[:, i, 0:HW],
                                eq[:, bass.ds(c + (Q * QC) % EQ_RING, 1), k,
                                   i * P:(i + 1) * P].rearrange("p o f -> p (o f)"),
                                h[:, bass.ds(c * TJ + (q * QC * TJ + k), 1), :].rearrange("p o f -> p (o f)"),
                                start=(first and k == 0), stop=(last and k == TJ - 1))
                    mm.then_inc(eq_used, 1)

                if q == 0:
                    chunk(0, first=True)
                with pe.Fori(1 if q == 0 else 0, QC - 1 if q == QUARTERS - 1 else QC) as c:
                    chunk(c)
                if q == QUARTERS - 1:
                    chunk(QC - 1, last=True)

            def attend(z):
                m, lo, hi = segments[z]
                s, first_block, end_block = strips[m]
                if lo == first_block:
                    if m >= 1:
                        pe.wait_ge(strip_taken, m)
                    pe.wait_ge(y_made, min(s + 1, BLOCKS) if m < LOWER else BLOCKS)

                def column_block(b, first=False, last=False):
                    for k in range(TJ):
                        pe.wait_ge(prob_made, b * TJ + (units_before[z] + k + 1))
                        for i in range(TJ):
                            mm = nc.tensor.matmul(
                                strip_out(i), prob[:, k, i * P:(i + 1) * P],
                                y[:, bass.ds(b * TJ + (lo * TJ + k), 1), :].rearrange("p o f -> p (o f)"),
                                start=(first and k == 0 and i % 2 == 0), stop=(last and k == TJ - 1),
                                skip_group_check=True)
                        mm.then_inc(prob_used, 1)

                is_first, is_last = lo == first_block, hi == end_block
                head, tail = (1 if is_first else 0), (hi - lo - 1 if is_last else hi - lo)
                if is_first and is_last and hi - lo == 1:
                    column_block(0, True, True)
                else:
                    if is_first:
                        column_block(0, first=True)
                    if tail - head == 1:
                        column_block(head)
                    elif tail > head:
                        with pe.Fori(head, tail) as b:
                            column_block(b)
                    if is_last:
                        column_block(hi - lo - 1, last=True)

            def turn(n):
                e, second = divmod(n, 2)
                pe.wait_ge(h1_made if second else agg_made, e + 1)
                if second:
                    pe.wait_ge(turn_taken, 2 * e + 1)
                elif e >= 1:
                    pe.wait_ge(u_made, e)
                else:
                    pe.wait_ge(norm_taken, 1)
                for i in range(TJ):
                    mm = nc.tensor.transpose(turn_ps[:, i * P:(i + 1) * P], agg[:, i, :], ident[:])
                mm.then_inc(turn_done, 1)

            def project(n):
                e, second = divmod(n, 2)
                pe.wait_ge(turn_taken, n + 1)
                if second:
                    pe.wait_ge(x1_made, e + 1)
                elif e >= 1:
                    pe.wait_ge(y_made, e)
                for i in range(TJ):
                    mm = nc.tensor.matmul(proj_ps[:, i * D:(i + 1) * D], feat_t[:, i, :],
                                          (w1_s if second else w0t_s)[:], start=True, stop=True)
                mm.then_inc(proj_done, 1)

            pe.wait_ge(ident_made, 1)
            for t in range(BLOCKS + 1):
                e = t - 1
                for q in range(QUARTERS):
                    if t < BLOCKS:
                        aggregate(t * QUARTERS + q)
                    if e >= 0 and q in (0, 2):
                        turn(2 * e + q // 2)
                    for z in segment_at.get((t, q), []):
                        attend(z)
                    if e >= 0 and q in (0, 2):
                        project(2 * e + q // 2)
                    if e >= 0 and q == 2:
                        nc.tensor.matmul(turn_ps[:], wa_rep[:, 0, :], feat_t[:].rearrange("p t f -> p (t f)"),
                                         start=True, stop=True).then_inc(turn_done, 1)
                    if t == 0 and q == 3:
                        pe.wait_ge(const_loaded, 16 * 5)
                        pe.wait_ge(wa_made, 1)
                        nc.tensor.matmul(turn_ps[:, 0:1], wa_rep[:, 1, :], wa[:, 1:2],
                                         start=True, stop=True).then_inc(norm_made, 1)
            for s in range(BLOCKS - 1, -1, -1):
                for z in segment_at.get(("upper", s), []):
                    attend(z)


def kernel(x, adj, L0_gnn_W, L0_gnn_b, L1_gnn_W, L1_gnn_a):
    import numpy as np
    import concourse.bacc as bacc
    from concourse.bass_utils import run_bass_kernel_spmd

    n, d = x.shape
    blocks, tj, p = 16, 4, 128
    chunks = n // (tj * p)
    blk = n // blocks
    a5 = np.ascontiguousarray(adj.reshape(blocks, blk, chunks, tj, p).transpose(0, 2, 4, 3, 1))
    arrays = {
        "in_x": np.ascontiguousarray(x).reshape(n // p, p, d),
        "in_adj": a5,
        "in_w0t": np.ascontiguousarray(L0_gnn_W.T),
        "in_b0": np.ascontiguousarray(L0_gnn_b),
        "in_w1": np.ascontiguousarray(L1_gnn_W),
        "in_a": np.ascontiguousarray(L1_gnn_a).reshape(2, d),
    }
    nc = bacc.Bacc("TRN2", target_bir_lowering=False, num_devices=1)
    args = [nc.dram_tensor(k, v.shape, mybir.dt.from_np(v.dtype), kind="ExternalInput").ap() for k, v in arrays.items()]
    out = nc.dram_tensor("out_rows", (n // p, p, d), F32, kind="ExternalOutput").ap()
    two_layer_gnn(nc, *args, out)
    r = run_bass_kernel_spmd(nc, [arrays], core_ids=[0])
    return r.results[0]["out_rows"].reshape(n, d)
```

```python
from contextlib import ExitStack

import concourse.bass as bass
from concourse import mybir

P = 128
LEAK = 0.2
LN_EPS = 1e-5
LIFT = 36.0
H_SCALE = 2048.0
GATE = 64.0

ALU = mybir.AluOpType
ACT = mybir.ActivationFunctionType
F32 = mybir.dt.float32
F16 = mybir.dt.float16
BF16 = mybir.dt.bfloat16
U8 = mybir.dt.uint8
I32 = mybir.dt.int32


def two_layer_gnn(nc, x, adj, w0t, b0, w1, a, out):
    D = x.shape[2]
    BLOCKS = adj.shape[0]
    CHUNKS = adj.shape[1]
    TJ = adj.shape[3]
    BLK = adj.shape[4]
    JT = CHUNKS * TJ
    QUARTERS = 4
    QC = CHUNKS // QUARTERS
    ADJ_RING = 6
    EQ_RING = 2 * QC
    GT_RING = 2 * QC
    SEG = 4
    UP_SEG = 8
    STATISTICS_AT = {(0, 1): 2, (0, 3): 3}
    NORMALIZE_AT = {(0, 0): 1, (1, 0): 2, (2, 0): 3}
    HIGH_AT = {(0, 0): 1, (1, 0): 2, (2, 0): 3}
    LOW_AT = {(0, 2): 1, (1, 1): 2, (2, 1): 3}
    HW = 2 * D + 1
    YW = D + 1
    NQ = BLOCKS * QUARTERS
    assert TJ * P == BLK and BLOCKS * TJ == JT and QC == 4 and BLOCKS == CHUNKS

    strips, segments, segment_at = [], [], {}

    def add_segment(lo, hi, when):
        if hi > lo:
            segment_at.setdefault(when, []).append(len(segments))
            segments.append((len(strips), lo, hi))

    for s in range(BLOCKS - 1):
        for q in range(QUARTERS):
            add_segment((s + 1) * q // QUARTERS, (s + 1) * (q + 1) // QUARTERS, (s + 2, q))
        strips.append((s, 0, s + 1))
    upper = [BLOCKS - 1]
    while len(upper) < BLOCKS:
        n = len(upper)
        upper.append((n - 1) // 2 if n % 2 else BLOCKS - 1 - n // 2)
    assert sorted(upper) == list(range(BLOCKS))
    for n, s in enumerate(upper):
        first = s + 1 if n else 0
        for lo in range(first, BLOCKS, UP_SEG):
            add_segment(lo, min(lo + UP_SEG, BLOCKS), ("upper", n))
        strips.append((s, first, BLOCKS))
    LOWER = BLOCKS - 1
    UPPER_SEGMENTS = [z for z, (m, _, _) in enumerate(segments) if m >= LOWER]

    def unpacked_upto(z):
        return z + 1 + max(0, z + 1 - UPPER_SEGMENTS[0])

    strip_last_segment = {m: z for z, (m, _, _) in enumerate(segments)}
    units_before, n = [], 0
    for _, lo, hi in segments:
        units_before.append(n)
        n += TJ * (hi - lo)
    units_upto_strip = {m: units_before[z] + TJ * (segments[z][2] - segments[z][1])
                        for m, z in strip_last_segment.items()}

    def row_slot(m):
        return (m if m < LOWER else m - LOWER + 1) % 2

    def times_loaded(n):
        return (n + 1) // 2

    gt_dram = nc.dram_tensor("gt_bits", [BLOCKS, P, CHUNKS, BLK], U8, kind="Internal").ap()
    r_dram = nc.dram_tensor("r_rows", [BLOCKS, P, BLK], F32, kind="Internal").ap()
    x1_dram = nc.dram_tensor("x1_rows", [BLOCKS, P, TJ, D], F32, kind="Internal").ap()
    low_dram = nc.dram_tensor("lower_sums", [BLOCKS, P, TJ, YW], F32, kind="Internal").ap()

    ctx = ExitStack()
    with ctx:
        def sb(name, shape, dt):
            return ctx.enter_context(nc.sbuf_tensor(name, shape, dt))

        def ps(name, shape):
            return ctx.enter_context(nc.psum_tensor(name, shape, F32))

        def sem(name):
            return ctx.enter_context(nc.semaphore(name))

        h = sb("h", [P, JT, HW], F16)
        y = sb("y", [P, JT, YW], F32)
        adj_in = sb("adj_in", [P, ADJ_RING, TJ, BLK], I32)
        eq = sb("eq", [P, EQ_RING, TJ, BLK], BF16)
        gt = sb("gt", [P, GT_RING, TJ, BLK], U8)
        bits_out = sb("bits_out", [P, 2, QC, BLK], U8)
        bits_in = sb("bits_in", [P, 2, SEG, BLK], U8)
        strip_mask = sb("strip_mask", [P, SEG, TJ, BLK], U8)
        prob = sb("prob", [P, TJ, BLK], F32)
        r_row = sb("r_row", [P, 2, BLK], F32)
        strip_sum = sb("strip_sum", [P, 2, TJ, YW], F32)
        low_in = sb("low_in", [P, 2, TJ, YW], F32)
        xb = sb("xb", [P, TJ, D], F32)
        x1 = sb("x1", [P, 2, TJ, D], F32)
        agg_raw = low_in[:].rearrange("p r t f -> p (r t f)")[:, 0:TJ * HW].rearrange("p (t f) -> p t f", t=TJ)
        agg = sb("agg", [P, TJ, D], F32)
        feat_t = sb("feat_t", [P, TJ, P], F32)
        stats = sb("stats", [P, JT, 6], F32)
        mean_var = sb("mean_var", [P, JT, 2], F32)
        rstd = sb("rstd", [P, JT], F32)
        rdeg = sb("rdeg", [P, TJ], F32)
        g_col = sb("g_col", [P, JT], F32)
        v_col = sb("v_col", [P, TJ], F32)
        fin_rec = sb("fin_rec", [P, 2, TJ], F32)
        ident = sb("ident", [P, P], F32)
        w0t_s = sb("w0t_s", [P, D], F32)
        w1_s = sb("w1_s", [P, D], F32)
        b_s = sb("b_s", [P, D], F32)
        a_s = sb("a_s", [P, 2, D], F32)
        wa = sb("wa", [P, 2], F32)
        wa_rep = sb("wa_rep", [P, 2, P], F32)
        ones = sb("ones", [P, P], F32)
        vmax = sb("vmax", [P, 1], F32)
        cst = sb("cst", [P, 6], F32)
        g_bias, f_bias, r_bias = cst[:, 0:1], cst[:, 1:2], cst[:, 2:3]
        gate_bias, eps, scaled_eps = cst[:, 3:4], cst[:, 4:5], cst[:, 5:6]
        adj_flat = adj_in[:].rearrange("p r t f -> p (r t f)").bitcast(U8)
        MASK_BYTES = UP_SEG * TJ * BLK
        up_mask = adj_flat[:, 0:2 * MASK_BYTES].rearrange("p (r b t f) -> p r b t f", r=2, b=UP_SEG, t=TJ)
        up_bits = adj_flat[:, 2 * MASK_BYTES:2 * MASK_BYTES + 2 * UP_SEG * BLK].rearrange(
            "p (r b f) -> p r b f", r=2, b=UP_SEG)

        def bits_of(z):
            m, lo, hi = segments[z]
            return (bits_in if m < LOWER else up_bits)[:, z % 2, 0:hi - lo, :]

        def mask_of(z):
            m, lo, hi = segments[z]
            return strip_mask[:, 0:hi - lo] if m < LOWER else up_mask[:, z % 2, 0:hi - lo]

        neg = feat_t
        pos = agg
        junk = agg

        bank = 512
        agg_ps = ps("agg_ps", [P, TJ, bank])
        strip_ps = ps("strip_ps", [P, 2, bank])
        turn_ps = ps("turn_ps", [P, bank])
        proj_ps = ps("proj_ps", [P, bank])

        def strip_banks(m):
            return strip_ps[:] if m < LOWER or (m - LOWER) % 2 == 0 else agg_ps[:, 0:2]

        def strip_out(m, i):
            return strip_banks(m)[:, i // 2, (i % 2) * YW:(i % 2 + 1) * YW]

        const_loaded = sem("const_loaded")
        x_loaded = [sem(f"x_loaded{q}") for q in range(QUARTERS)]
        adj_loaded = [sem(f"adj_loaded{r}") for r in range(ADJ_RING)]
        bits_stored = [sem(f"bits_stored{r}") for r in range(2)]
        bits_loaded = [sem(f"bits_loaded{r}") for r in range(2)]
        xblk_loaded = sem("xblk_loaded")
        rows_stored = [sem(f"rows_stored{r}") for r in range(2)]
        sums_stored = [sem(f"sums_stored{r}") for r in range(2)]
        r_loaded = [sem(f"r_loaded{r}") for r in range(2)]
        rest_loaded = [sem(f"rest_loaded{r}") for r in range(2)]
        out_stored = sem("out_stored")
        ident_zero = sem("ident_zero")
        ident_made = sem("ident_made")
        xb_made = sem("xb_made")
        cst_made = sem("cst_made")
        ln_stat = sem("ln_stat")
        ln_std = sem("ln_std")
        ln_inv = sem("ln_inv")
        ln_made = sem("ln_made")
        ln_high = sem("ln_high")
        h_made = sem("h_made")
        wa_made = sem("wa_made")
        norm_made = sem("norm_made")
        norm_taken = sem("norm_taken")
        vmax_made = sem("vmax_made")
        dve_step = sem("dve_step")
        pool_step = sem("pool_step")
        eq_made = sem("eq_made")
        gt_made = sem("gt_made")
        pairs_made = sem("pairs_made")
        bits_made = sem("bits_made")
        masks_made = sem("masks_made")
        eq_used = sem("eq_used")
        agg_taken = sem("agg_taken")
        agg_made = sem("agg_made")
        turn_done = sem("turn_done")
        turn_taken = sem("turn_taken")
        proj_done = sem("proj_done")
        x1_made = sem("x1_made")
        dev_ready = sem("dev_ready")
        std_made = sem("std_made")
        h1_made = sem("h1_made")
        v_made = sem("v_made")
        gf_made = sem("gf_made")
        u_made = sem("u_made")
        y_made = sem("y_made")
        r_made = sem("r_made")
        prob_made = sem("prob_made")
        prob_used = sem("prob_used")
        strip_taken = sem("strip_taken")
        rec_made = sem("rec_made")
        neg_made = sem("neg_made")
        exp_made = sem("exp_made")
        out_made = sem("out_made")

        block = ctx.enter_context(nc.Block())

        @block.sync
        def _(sp):
            def load_adj(g):
                if g >= ADJ_RING:
                    sp.wait_ge(eq_made, g - ADJ_RING + 1)
                    sp.wait_ge(gt_made, g - ADJ_RING + 1)
                sp.dma_start(adj_in[:, g % ADJ_RING], adj[g // CHUNKS, g % CHUNKS])\
                  .then_inc(adj_loaded[g % ADJ_RING], 16)

            def store_bits(Q):
                t, q = divmod(Q, QUARTERS)
                sp.wait_ge(bits_made, Q + 1)
                sp.dma_start(gt_dram[t, :, q * QC:(q + 1) * QC, :], bits_out[:, Q % 2])\
                  .then_inc(bits_stored[Q % 2], 16)

            def load_bits(z):
                m, lo, hi = segments[z]
                s = strips[m][0]
                for r in range(2):
                    sp.wait_ge(bits_stored[r], 16 * (s + 1) * QUARTERS // 2)
                if z >= 2:
                    sp.wait_ge(masks_made, unpacked_upto(z - 2))
                if m == LOWER:
                    sp.wait_ge(eq_made, BLOCKS * CHUNKS)
                    sp.wait_ge(gt_made, BLOCKS * CHUNKS)
                sp.dma_start(bits_of(z), gt_dram[s, :, lo:hi, :])\
                  .then_inc(bits_loaded[z % 2], 16)

            def load_x_block(t):
                if t >= 1:
                    sp.wait_ge(x1_made, t)
                sp.dma_start(xb[:], x[t * TJ:(t + 1) * TJ].rearrange("t p d -> p t d")).then_inc(xblk_loaded, 16)

            def store_rows(t):
                sp.wait_ge(x1_made, t + 1)
                sp.dma_start(x1_dram[t], x1[:, t % 2]).then_inc(rows_stored[t % 2], 16)
                sp.wait_ge(r_made, t + 1)
                sp.dma_start(r_dram[t], r_row[:, t % 2, :]).then_inc(rows_stored[t % 2], 16)

            def store_sums(s):
                sp.wait_ge(strip_taken, s + 1)
                sp.dma_start(low_dram[s], strip_sum[:, s % 2]).then_inc(sums_stored[s % 2], 16)

            def load_r(n):
                m = LOWER + n
                for r in range(2):
                    sp.wait_ge(rows_stored[r], 32 * BLOCKS // 2)
                sp.wait_ge(prob_made, units_upto_strip[m - 2])
                sp.dma_start(r_row[:, row_slot(m), :], r_dram[upper[n]]).then_inc(r_loaded[row_slot(m)], 16)

            def load_rest(n):
                slot = row_slot(LOWER + n)
                if n >= 2:
                    sp.wait_ge(out_made, n - 1)
                for r in range(2):
                    sp.wait_ge(sums_stored[r], 16 * ((LOWER + 1 - r) // 2))
                sp.dma_start(x1[:, slot], x1_dram[upper[n]]).then_inc(rest_loaded[slot], 16)
                sp.dma_start(low_in[:, slot], low_dram[upper[n]]).then_inc(rest_loaded[slot], 16)

            def store_out(n):
                s = upper[n]
                sp.wait_ge(out_made, n + 1)
                sp.dma_start(out[s * TJ:(s + 1) * TJ].rearrange("t p d -> p t d"), pos[:]).then_inc(out_stored, 16)

            for g in range(ADJ_RING + QC):
                load_adj(g)
            for t in range(BLOCKS + 1):
                for q in range(QUARTERS):
                    Q = t * QUARTERS + q
                    for z in segment_at.get(divmod(Q + 1, QUARTERS), []):
                        load_bits(z)
                    for g in range((Q + 1) * QC + ADJ_RING, (Q + 2) * QC + ADJ_RING):
                        if g < BLOCKS * CHUNKS:
                            load_adj(g)
                    if t < BLOCKS:
                        store_bits(Q)
                    if q == 3 and t < BLOCKS:
                        load_x_block(t)
                    if q == 0 and t >= 2:
                        store_rows(t - 2)
                    if q == 1 and t >= 3:
                        store_sums(t - 3)
            for n in range(BLOCKS):
                if n >= 1:
                    load_r(n)
                for z in segment_at["upper", n]:
                    load_bits(z)
                if n == 0:
                    store_rows(BLOCKS - 1)
                    store_sums(LOWER - 1)
                else:
                    load_rest(n)
                if n >= 2:
                    store_out(n - 2)
            store_out(BLOCKS - 2)
            store_out(BLOCKS - 1)
            sp.wait_ge(out_stored, 16 * BLOCKS)

        @block.gpsimd
        def _(pool):
            nc.gpsimd.memset(ident[:], 0.0).then_inc(ident_zero, 1)
            nc.gpsimd.memset(ones[:], 1.0).then_inc(ident_zero, 1)
            nc.gpsimd.memset(h[:, :, 2 * D:HW], H_SCALE).then_inc(ident_zero, 1)
            nc.gpsimd.memset(cst[:, 2:3], LIFT).then_inc(ident_zero, 1)
            nc.gpsimd.memset(cst[:, 3:4], -GATE / 2).then_inc(ident_zero, 1)
            nc.gpsimd.memset(cst[:, 4:5], LN_EPS).then_inc(ident_zero, 1)
            nc.gpsimd.memset(cst[:, 5:6], LN_EPS / H_SCALE ** 2).then_inc(ident_zero, 1)
            pool.wait_ge(ident_zero, 7)
            nc.gpsimd.affine_select(out=ident[:], in_=ident[:], compare_op=ALU.not_equal, fill=1.0, base=0,
                                    pattern=[[-1, P]], channel_multiplier=1).then_inc(ident_made, 1)
            pool.wait_ge(const_loaded, 16 * 5)
            links = [0]

            def link(instruction):
                links[0] += 1
                instruction.then_inc(pool_step, 1)
                pool.wait_ge(pool_step, links[0])

            for t in range(BLOCKS):
                pool.wait_ge(xblk_loaded, 16 * (t + 1))
                for i in range(TJ):
                    last = nc.gpsimd.tensor_tensor(xb[:, i, :], xb[:, i, :], b_s[:], ALU.add)
                last.then_inc(xb_made, 1)
                pool.wait_ge(agg_taken, t + 1)
                if t >= 1:
                    pool.wait_ge(turn_done, 3 * t - 1)
                    pool.wait_ge(v_made, t)
                nc.gpsimd.tensor_tensor(agg[:], agg_raw[:, :, 0:D], agg_raw[:, :, D:2 * D],
                                        ALU.add).then_inc(agg_made, 1)

            for n in range(BLOCKS):
                slot = row_slot(LOWER + n)
                if n == 0:
                    pool.wait_ge(rows_stored[slot], 32 * BLOCKS // 2)
                else:
                    pool.wait_ge(rest_loaded[slot], 32 * times_loaded(n))
                link(nc.gpsimd.tensor_scalar(x1[:, slot], x1[:, slot], -1.0, None, ALU.add))
                pool.wait_ge(exp_made, n + 1)
                link(nc.gpsimd.tensor_tensor(pos[:], pos[:], x1[:, slot], ALU.add))
                nc.gpsimd.tensor_tensor(pos[:], pos[:], neg[:], ALU.add).then_inc(out_made, 1)

        @block.scalar
        def _(act):
            for q in range(QUARTERS):
                n = JT // QUARTERS
                act.dma_start(y[:, q * n:(q + 1) * n, 0:D],
                              x[q * n:(q + 1) * n].rearrange("t p d -> p t d")).then_inc(x_loaded[q], 16)
            act.dma_start(w1_s[:], w1).then_inc(const_loaded, 16)
            act.dma_start(w0t_s[:], w0t).then_inc(const_loaded, 16)
            act.dma_start(b_s[:], b0.partition_broadcast(P)).then_inc(const_loaded, 16)
            act.dma_start(a_s[:, 0, :], a[0].partition_broadcast(P)).then_inc(const_loaded, 16)
            act.dma_start(a_s[:, 1, :], a[1].partition_broadcast(P)).then_inc(const_loaded, 16)
            act.wait_ge(ident_made, 1)

            def gate(Q, p):
                g = Q * QC + p
                if Q < NQ:
                    act.wait_ge(adj_loaded[g % ADJ_RING], 16 * (g // ADJ_RING + 1))
                    if Q >= 2:
                        act.wait_ge(bits_made, Q - 1)
                    nc.scalar.activation(gt[:, g % GT_RING], adj_in[:, g % ADJ_RING], ACT.Sigmoid,
                                         bias=gate_bias, scale=GATE).then_inc(gt_made, 1)

            def ln_std_of(q):
                n = JT // QUARTERS
                j = slice(q * n, (q + 2) * n)
                act.wait_ge(ln_stat, q + 2)
                nc.scalar.activation(rstd[:, j], mean_var[:, j, 1], ACT.Sqrt, bias=scaled_eps,
                                     scale=H_SCALE ** -2).then_inc(ln_std, 1)

            def high_half(q):
                n = JT // QUARTERS
                j = slice(q * n, (q + 1) * n)
                act.wait_ge(ln_made, q + 1)
                nc.scalar.activation(h[:, j, 0:D], y[:, j, 0:D], ACT.Relu).then_inc(ln_high, 1)

            def take_strip(m):
                act.wait_ge(prob_used, units_upto_strip[m])
                if 2 <= m < LOWER + 2:
                    act.wait_ge(sums_stored[m % 2], 16 * (m // 2))
                if m >= LOWER + 2:
                    act.wait_ge(out_made, m - LOWER - 1)
                for b in range(2):
                    last = nc.scalar.activation(strip_sum[:, m % 2, 2 * b:2 * b + 2, :],
                                                strip_banks(m)[:, b, 0:2 * YW].rearrange("p (t f) -> p t f", t=2),
                                                ACT.Copy)
                last.then_inc(strip_taken, 1)

            def elu_parts(n):
                m = LOWER + n
                act.wait_ge(rec_made, n + 1)
                if n >= 1:
                    act.wait_ge(out_stored, 16 * n)
                for i in range(TJ):
                    last = nc.scalar.activation(neg[:, i, :], strip_sum[:, m % 2, i, 0:D], ACT.Relu,
                                                scale=fin_rec[:, 1, i:i + 1])
                last.then_inc(neg_made, 1)
                for i in range(TJ):
                    nc.scalar.activation(pos[:, i, :], strip_sum[:, m % 2, i, 0:D], ACT.Relu,
                                         scale=fin_rec[:, 0, i:i + 1])
                act.wait_ge(neg_made, n + 1)
                nc.scalar.activation(neg[:], neg[:], ACT.Exp, scale=-1.0).then_inc(exp_made, 1)

            def take_turn(n):
                t, second = divmod(n, 2)
                act.wait_ge(turn_done, 3 * t + second + 1)
                if second == 0 and t >= 1:
                    act.wait_ge(turn_done, 3 * t)
                if second == 1:
                    act.wait_ge(proj_done, 2 * t + 1)
                nc.scalar.activation(feat_t[:].rearrange("p t f -> p (t f)"), turn_ps[:],
                                     ACT.Relu if second else ACT.Copy).then_inc(turn_taken, 1)

            def take_sums(t):
                act.wait_ge(eq_used, CHUNKS * (t + 1))
                if t >= 1:
                    act.wait_ge(agg_made, t)
                    act.wait_ge(x1_made, t)
                nc.scalar.activation(agg_raw, agg_ps[:, :, 0:HW], ACT.Copy).then_inc(agg_taken, 1)

            def std(e):
                act.wait_ge(dev_ready, e + 1)
                nc.scalar.activation(rstd[:, 0:TJ], mean_var[:, 0:TJ, 1], ACT.Sqrt, bias=eps).then_inc(std_made, 1)

            def factors(e):
                if e == 0:
                    act.wait_ge(vmax_made, 2)
                js = slice(e * TJ, (e + 1) * TJ)
                act.wait_ge(v_made, e + 1)
                nc.scalar.activation(g_col[:, js], v_col[:], ACT.Exp, bias=g_bias, scale=1.0 - LEAK)
                nc.scalar.activation(y[:, js, D], v_col[:], ACT.Exp, bias=f_bias, scale=LEAK).then_inc(gf_made, 1)
                act.wait_ge(turn_done, 3 * e + 3)
                if e >= 2:
                    act.wait_ge(rows_stored[e % 2], 32 * (e // 2))
                    act.wait_ge(prob_made, units_upto_strip[e - 2])
                nc.scalar.activation(r_row[:, e % 2, :], turn_ps[:], ACT.Relu, bias=vmax[:, 0:1]).then_inc(u_made, 1)
                act.wait_ge(u_made, e + 1)
                nc.scalar.activation(r_row[:, e % 2, :], r_row[:, e % 2, :], ACT.Exp, bias=r_bias,
                                     scale=LEAK - 1.0).then_inc(r_made, 1)
                act.wait_ge(gf_made, e + 1)
                for i in range(TJ):
                    last = nc.scalar.activation(y[:, e * TJ + i, 0:D], proj_ps[:, i * D:(i + 1) * D],
                                                ACT.Copy, scale=y[:, e * TJ + i, D:YW])
                last.then_inc(y_made, 1)

            ln_std_of(0)
            for p in range(QC):
                gate(0, p)
                if p == 0:
                    high_half(0)
            for t in range(BLOCKS + 1):
                e = t - 1
                for q in range(QUARTERS):
                    Q = t * QUARTERS + q
                    if q == 0 and e >= 0:
                        take_sums(e)
                    if q == 0 and t >= 3:
                        take_strip(t - 3)
                    if q == 1 and e >= 0:
                        take_turn(2 * e)
                    if q == 3 and e >= 0:
                        take_turn(2 * e + 1)
                    for p in range(QC):
                        gate(Q + 1, p)
                        if t == 0 and (q, p) in HIGH_AT:
                            high_half(HIGH_AT[q, p])
                        if t == 0 and (q, p) == (0, 3):
                            ln_std_of(2)
                    if q == 2 and e >= 0:
                        std(e)
                    if q == 3 and e >= 0:
                        factors(e)
                    if q == 3 and t == 0:
                        act.wait_ge(norm_made, 1)
                        nc.scalar.activation(vmax[:], turn_ps[:, 0:1], ACT.Sqrt, scale=float(D))\
                          .then_inc(norm_taken, 1)
            take_strip(LOWER - 1)
            for n in range(BLOCKS):
                if n >= 1:
                    elu_parts(n - 1)
                take_strip(LOWER + n)
            elu_parts(BLOCKS - 1)

        @block.vector
        def _(dve):
            links = [0]

            def link(instruction):
                links[0] += 1
                instruction.then_inc(dve_step, 1)
                dve.wait_ge(dve_step, links[0])

            def statistics(q):
                n = JT // QUARTERS
                dve.wait_ge(x_loaded[q], 16)
                for j in range(q * n, (q + 1) * n):
                    last = nc.vector.bn_stats(stats[:, j, :], y[:, j, 0:D])
                link(last)
                for j in range(q * n, (q + 1) * n):
                    last = nc.vector.bn_aggr(mean_var[:, j, :], stats[:, j, :])
                last.then_inc(ln_stat, 1)

            def invert_std(q):
                js = slice(q * (JT // QUARTERS), (q + 2) * (JT // QUARTERS))
                dve.wait_ge(ln_std, q // 2 + 1)
                nc.vector.reciprocal(rstd[:, js], rstd[:, js]).then_inc(ln_inv, 1)

            def normalize(q):
                n = JT // QUARTERS
                dve.wait_ge(ln_stat, q + 1)
                dve.wait_ge(ln_inv, q // 2 + 1)
                for j in range(q * n, (q + 1) * n):
                    last = nc.vector.tensor_scalar(y[:, j, 0:D], y[:, j, 0:D], mean_var[:, j, 0:1],
                                                   rstd[:, j:j + 1], ALU.subtract, ALU.mult)
                last.then_inc(ln_made, 1)

            def low_half(q):
                n = JT // QUARTERS
                js = slice(q * n, (q + 1) * n)
                dve.wait_ge(ln_made, q + 1)
                dve.wait_ge(ln_high, q + 1)
                nc.vector.scalar_tensor_tensor(out=h[:, js, D:2 * D], in0=y[:, js, 0:D], scalar=0.0,
                                               in1=h[:, js, 0:D], op0=ALU.max, op1=ALU.subtract)\
                    .then_inc(h_made, 1)

            def equal(Q, p):
                g = Q * QC + p
                if Q < NQ:
                    dve.wait_ge(adj_loaded[g % ADJ_RING], 16 * (g // ADJ_RING + 1))
                    if g >= EQ_RING:
                        dve.wait_ge(eq_used, g - EQ_RING + 1)
                    nc.vector.tensor_scalar(eq[:, g % EQ_RING], adj_in[:, g % ADJ_RING], 1.0, None,
                                            ALU.is_equal).then_inc(eq_made, 1)

            def pack(Q):
                dve.wait_ge(gt_made, QC * (Q + 1))
                if Q >= 2:
                    dve.wait_ge(bits_stored[Q % 2], 16 * (Q // 2))
                half = slice((Q % 2) * QC, (Q % 2 + 1) * QC)
                g4 = gt[:, half].rearrange("p c (h k) f -> p (c h) k f", k=2).bitcast(I32)
                nc.vector.scalar_tensor_tensor(out=g4[:, :, 0, :], in0=g4[:, :, 0, :], scalar=1, in1=g4[:, :, 1, :],
                                               op0=ALU.logical_shift_left,
                                               op1=ALU.bitwise_or).then_inc(pairs_made, 1)
                dve.wait_ge(pairs_made, Q + 1)
                g2 = gt[:, half].bitcast(I32)
                nc.vector.scalar_tensor_tensor(out=bits_out[:, Q % 2].bitcast(I32), in0=g2[:, :, 0, :], scalar=2,
                                               in1=g2[:, :, 2, :], op0=ALU.logical_shift_left,
                                               op1=ALU.bitwise_or).then_inc(bits_made, 1)

            def unpack(z):
                m, lo, hi = segments[z]
                s = strips[m][0]
                dve.wait_ge(bits_loaded[z % 2], 16 * (z // 2 + 1))
                reused = z - 1 if m < LOWER else z - 2
                if m >= LOWER and reused < UPPER_SEGMENTS[0]:
                    dve.wait_ge(gt_made, BLOCKS * CHUNKS)
                    dve.wait_ge(eq_made, BLOCKS * CHUNKS)
                elif reused >= 0:
                    dve.wait_ge(prob_made, units_before[reused + 1])
                unpack_tiles(z, range(TJ) if m < LOWER else range(TJ // 2))

            def unpack_tiles(z, tiles):
                for k in tiles:
                    last = nc.vector.tensor_scalar(
                        mask_of(z)[:, :, k, :].bitcast(I32), bits_of(z).bitcast(I32),
                        TJ - 1 - k, 0x01010101, ALU.logical_shift_right, ALU.bitwise_and)
                last.then_inc(masks_made, 1)

            def unpack_rest(z):
                unpack_tiles(z, range(TJ // 2, TJ))

            def weights(z, b):
                m, lo, hi = segments[z]
                s = strips[m][0]
                if isinstance(b, int) and b == 0:
                    if m <= LOWER:
                        dve.wait_ge(r_made, s + 1)
                    else:
                        dve.wait_ge(r_loaded[row_slot(m)], 16 * times_loaded(m - LOWER))
                    dve.wait_ge(masks_made, unpacked_upto(z))
                for k in range(TJ):
                    if units_before[z] > 0 or (isinstance(b, int) and b > 0):
                        dve.wait_ge(prob_used, b * TJ + (units_before[z] + k - TJ + 1))
                    nc.vector.scalar_tensor_tensor(
                        out=prob[:, k, :], in0=r_row[:, row_slot(m), :],
                        scalar=g_col[:, bass.ds(b * TJ + (lo * TJ + k), 1)],
                        in1=mask_of(z)[:, bass.ds(b, 1), k, :].rearrange("p o f -> p (o f)"),
                        op0=ALU.max, op1=ALU.mult).then_inc(prob_made, 1)

            def residual_norm(e):
                dve.wait_ge(agg_made, e + 1)
                link(nc.vector.reciprocal(rdeg[:], agg_raw[:, :, 2 * D]))
                dve.wait_ge(proj_done, 2 * e + 1)
                dve.wait_ge(xb_made, e + 1)
                if e >= 2:
                    dve.wait_ge(rows_stored[e % 2], 32 * (e // 2))
                for i in range(TJ):
                    last = nc.vector.scalar_tensor_tensor(out=x1[:, e % 2, i, :], in0=proj_ps[:, i * D:(i + 1) * D],
                                                          scalar=rdeg[:, i:i + 1], in1=xb[:, i, :],
                                                          op0=ALU.mult, op1=ALU.add)
                last.then_inc(x1_made, 1)
                dve.wait_ge(x1_made, e + 1)
                for i in range(TJ):
                    last = nc.vector.bn_stats(stats[:, i, :], x1[:, e % 2, i, :])
                link(last)
                for i in range(TJ):
                    last = nc.vector.bn_aggr(mean_var[:, i, :], stats[:, i, :])
                last.then_inc(dev_ready, 1)

            def second_norm(e):
                dve.wait_ge(dev_ready, e + 1)
                dve.wait_ge(std_made, e + 1)
                link(nc.vector.reciprocal(rstd[:, 0:TJ], rstd[:, 0:TJ]))
                for i in range(TJ):
                    last = nc.vector.tensor_scalar(agg[:, i, :], x1[:, e % 2, i, :], mean_var[:, i, 0:1],
                                                   rstd[:, i:i + 1], ALU.subtract, ALU.mult)
                last.then_inc(h1_made, 1)

            def logits(e):
                dve.wait_ge(proj_done, 2 * e + 2)
                if e >= 1:
                    dve.wait_ge(gf_made, e)
                for i in range(TJ):
                    last = nc.vector.tensor_tensor_reduce(junk[:, i, :], proj_ps[:, i * D:(i + 1) * D], a_s[:, 1, :],
                                                          1.0, 0.0, ALU.mult, ALU.add, v_col[:, i:i + 1])
                last.then_inc(v_made, 1)

            def invert(n):
                m = LOWER + n
                dve.wait_ge(strip_taken, m + 1)
                total = strip_sum[:, m % 2]
                if n >= 1:
                    dve.wait_ge(rest_loaded[row_slot(m)], 32 * times_loaded(n))
                    link(nc.vector.tensor_tensor(total, total, low_in[:, row_slot(m)], ALU.add))
                    dve.wait_ge(exp_made, n)
                link(nc.vector.reciprocal(fin_rec[:, 0, :], total[:, :, D]))
                nc.vector.tensor_scalar(fin_rec[:, 1, :], fin_rec[:, 0, :], -1.0, None,
                                        ALU.mult).then_inc(rec_made, 1)

            statistics(0)
            equal(0, 0)
            statistics(1)
            equal(0, 1)
            invert_std(0)
            normalize(0)
            equal(0, 2)
            low_half(0)
            equal(0, 3)
            for t in range(BLOCKS + 1):
                e = t - 1
                for q in range(QUARTERS):
                    Q = t * QUARTERS + q
                    z = segment_at.get((t, q), [None])[0]
                    blocks = 0 if z is None else segments[z][2] - segments[z][1]
                    for p in range(QC):
                        equal(Q + 1, p)
                        if t == 0:
                            if (q, p) in STATISTICS_AT:
                                statistics(STATISTICS_AT[q, p])
                            if (q, p) == (1, 0):
                                invert_std(2)
                            if (q, p) in NORMALIZE_AT:
                                normalize(NORMALIZE_AT[q, p])
                            if (q, p) in LOW_AT:
                                low_half(LOW_AT[q, p])
                        if e >= 0:
                            if (q, p) == (2, 0):
                                residual_norm(e)
                            if (q, p) == (2, 2):
                                second_norm(e)
                            if (q, p) == (3, 3):
                                logits(e)
                        if p == 0 and blocks:
                            unpack(z)
                        if p == 2 and t < BLOCKS:
                            pack(Q)
                        if p < blocks:
                            weights(z, p)
                    if t == 0 and q == 3:
                        dve.wait_ge(const_loaded, 16 * 5)
                        for k in range(2):
                            link(nc.vector.tensor_tensor_reduce(junk[:, k, :], w1_s[:], a_s[:, k, :], 1.0, 0.0,
                                                                ALU.mult, ALU.add, wa[:, k:k + 1]))
                            last = nc.vector.tensor_scalar(wa_rep[:, k, :], ones[:], wa[:, k:k + 1], None, ALU.mult)
                        last.then_inc(wa_made, 1)
                        dve.wait_ge(norm_taken, 1)
                        nc.vector.tensor_scalar(cst[:, 0:1], vmax[:], LEAK - 1.0, LIFT, ALU.mult,
                                                ALU.add).then_inc(vmax_made, 1)
                        nc.vector.tensor_scalar(cst[:, 1:2], vmax[:], -LEAK, LIFT, ALU.mult,
                                                ALU.add).then_inc(vmax_made, 1)
            unpack(UPPER_SEGMENTS[0])
            unpack_rest(UPPER_SEGMENTS[0])
            for z in UPPER_SEGMENTS:
                m, lo, hi = segments[z]
                s = strips[m][0]
                following = z + 1 if z + 1 < len(segments) else None
                n = hi - lo
                before = m - LOWER - 1 if lo == strips[m][1] and m > LOWER else None
                if n > 1:
                    weights(z, 0)
                    if before is not None:
                        invert(before)
                if n > 3:
                    with dve.Fori(1, n - 1) as b:
                        weights(z, b)
                else:
                    for b in range(1, n - 1):
                        weights(z, b)
                if following is not None:
                    unpack(following)
                weights(z, n - 1)
                if following is not None:
                    unpack_rest(following)
                if n == 1 and before is not None:
                    invert(before)
            invert(BLOCKS - 1)

        @block.tensor
        def _(pe):
            def aggregate(Q, c, first=False, last=False):
                q = Q % QUARTERS
                pe.wait_ge(eq_made, c + (Q * QC + 1))
                for k in range(TJ):
                    for i in range(TJ):
                        mm = nc.tensor.matmul(
                            agg_ps[:, i, 0:HW],
                            eq[:, bass.ds(c + (Q * QC) % EQ_RING, 1), k,
                               i * P:(i + 1) * P].rearrange("p o f -> p (o f)"),
                            h[:, bass.ds(c * TJ + (q * QC * TJ + k), 1), :].rearrange("p o f -> p (o f)"),
                            start=(first and k == 0), stop=(last and k == TJ - 1))
                mm.then_inc(eq_used, 1)

            def attend(z, b, first=False, last=False):
                m, lo, _ = segments[z]
                for k in range(TJ):
                    pe.wait_ge(prob_made, b * TJ + (units_before[z] + k + 1))
                    for i in range(TJ):
                        mm = nc.tensor.matmul(
                            strip_out(m, i), prob[:, k, i * P:(i + 1) * P],
                            y[:, bass.ds(b * TJ + (lo * TJ + k), 1), :].rearrange("p o f -> p (o f)"),
                            start=(first and k == 0 and i % 2 == 0), stop=(last and k == TJ - 1),
                            skip_group_check=True)
                    mm.then_inc(prob_used, 1)

            def quarter(Q, z, middle):
                chunks = 0 if Q is None else QC
                blocks = 0 if z is None else segments[z][2] - segments[z][1]
                ends = {}
                if Q is not None:
                    if Q < QUARTERS:
                        pe.wait_ge(h_made, Q + 1)
                    if Q % QUARTERS == 0:
                        ends.setdefault(0, {})["agg_first"] = True
                        if Q:
                            pe.wait_ge(agg_taken, Q // QUARTERS)
                    if Q % QUARTERS == QUARTERS - 1:
                        ends.setdefault(QC - 1, {})["agg_last"] = True
                if z is not None:
                    m, lo, hi = segments[z]
                    s, first_block, end_block = strips[m]
                    if lo == first_block:
                        ends.setdefault(0, {})["strip_first"] = True
                    if hi == end_block:
                        ends.setdefault(blocks - 1, {})["strip_last"] = True

                def position(p, has_block, end):
                    if chunks:
                        aggregate(Q, p, end.get("agg_first", False), end.get("agg_last", False))
                    if has_block:
                        if "strip_first" in end:
                            if m == LOWER + 1:
                                pe.wait_ge(agg_taken, BLOCKS)
                            elif m >= 1:
                                pe.wait_ge(strip_taken, m if m <= LOWER else m - 1)
                            pe.wait_ge(y_made, s + 1 if m < LOWER else BLOCKS)
                        attend(z, p, "strip_first" in end, "strip_last" in end)

                p, total = 0, max(chunks, blocks)
                while p < total:
                    if middle and p == total // 2:
                        middle()
                    stop = p + 1
                    while stop < total and not chunks and p not in ends and stop not in ends and (stop < blocks) == (p < blocks) \
                            and not (middle and stop == total // 2):
                        stop += 1
                    if stop - p == 1:
                        position(p, p < blocks, ends.get(p, {}))
                    else:
                        with pe.Fori(p, stop) as c:
                            position(c, p < blocks, {})
                    p = stop

            def turn(n):
                e, second = divmod(n, 2)
                pe.wait_ge(h1_made if second else agg_made, e + 1)
                if second:
                    pe.wait_ge(turn_taken, 2 * e + 1)
                elif e >= 1:
                    pe.wait_ge(u_made, e)
                else:
                    pe.wait_ge(norm_taken, 1)
                for i in range(TJ):
                    mm = nc.tensor.transpose(turn_ps[:, i * P:(i + 1) * P], agg[:, i, :], ident[:])
                mm.then_inc(turn_done, 1)

            def project(n):
                e, second = divmod(n, 2)
                pe.wait_ge(turn_taken, n + 1)
                if second:
                    pe.wait_ge(x1_made, e + 1)
                elif e >= 1:
                    pe.wait_ge(y_made, e)
                for i in range(TJ):
                    mm = nc.tensor.matmul(proj_ps[:, i * D:(i + 1) * D], feat_t[:, i, :],
                                          (w1_s if second else w0t_s)[:], start=True, stop=True)
                mm.then_inc(proj_done, 1)

            pe.wait_ge(ident_made, 1)
            for t in range(BLOCKS + 1):
                e = t - 1
                for q in range(QUARTERS):
                    z = segment_at.get((t, q), [None])[0]

                    def project_first():
                        project(2 * e)

                    def project_second():
                        project(2 * e + 1)
                        nc.tensor.matmul(turn_ps[:], wa_rep[:, 0, :], feat_t[:].rearrange("p t f -> p (t f)"),
                                         start=True, stop=True).then_inc(turn_done, 1)

                    middle = {1: project_first, 3: project_second}.get(q) if e >= 0 else None
                    quarter(t * QUARTERS + q if t < BLOCKS else None, z, middle)
                    if e >= 0 and q in (0, 2):
                        turn(2 * e + q // 2)
                    if t == 0 and q == 3:
                        pe.wait_ge(const_loaded, 16 * 5)
                        pe.wait_ge(wa_made, 1)
                        nc.tensor.matmul(turn_ps[:, 0:1], wa_rep[:, 1, :], wa[:, 1:2],
                                         start=True, stop=True).then_inc(norm_made, 1)
            for z in UPPER_SEGMENTS:
                quarter(None, z, None)


def kernel(x, adj, L0_gnn_W, L0_gnn_b, L1_gnn_W, L1_gnn_a):
    import numpy as np
    import concourse.bacc as bacc
    from concourse.bass_utils import run_bass_kernel_spmd

    n, d = x.shape
    blocks, tj, p = 16, 4, 128
    chunks = n // (tj * p)
    blk = n // blocks
    a5 = np.ascontiguousarray(adj.reshape(blocks, blk, chunks, tj, p).transpose(0, 2, 4, 3, 1))
    arrays = {
        "in_x": np.ascontiguousarray(x).reshape(n // p, p, d),
        "in_adj": a5,
        "in_w0t": np.ascontiguousarray(L0_gnn_W.T),
        "in_b0": np.ascontiguousarray(L0_gnn_b),
        "in_w1": np.ascontiguousarray(L1_gnn_W),
        "in_a": np.ascontiguousarray(L1_gnn_a).reshape(2, d),
    }
    nc = bacc.Bacc("TRN2", target_bir_lowering=False, num_devices=1,
                   dynamic_dma_scratch_size=4096)
    args = [nc.dram_tensor(k, v.shape, mybir.dt.from_np(v.dtype), kind="ExternalInput").ap() for k, v in arrays.items()]
    out = nc.dram_tensor("out_rows", (n // p, p, d), F32, kind="ExternalOutput").ap()
    two_layer_gnn(nc, *args, out)
    r = run_bass_kernel_spmd(nc, [arrays], core_ids=[0])
    return r.results[0]["out_rows"].reshape(n, d)
```

```python
from contextlib import ExitStack

import concourse.bass as bass
from concourse import mybir

P = 128
LEAK = 0.2
LN_EPS = 1e-5
LIFT = 36.0
H_SCALE = 2048.0
GATE = 64.0

ALU = mybir.AluOpType
ACT = mybir.ActivationFunctionType
F32 = mybir.dt.float32
F16 = mybir.dt.float16
BF16 = mybir.dt.bfloat16
U8 = mybir.dt.uint8
I32 = mybir.dt.int32


def two_layer_gnn(nc, x, adj, w0t, b0, w1, a, out):
    D = x.shape[2]
    BLOCKS = adj.shape[0]
    CHUNKS = adj.shape[1]
    TJ = adj.shape[3]
    BLK = adj.shape[4]
    JT = CHUNKS * TJ
    QUARTERS = 4
    QC = CHUNKS // QUARTERS
    ADJ_RING = 6
    EQ_RING = 2 * QC
    GT_RING = 2 * QC
    SEG = 4
    UP_SEG = 8
    STATISTICS_AT = {(0, 1): 2, (0, 3): 3}
    NORMALIZE_AT = {(1, 1): 2}
    HIGH_AT = {(0, 0): 1, (1, 2): 2, (2, 0): 3}
    LOW_AT = {(0, 2): 1, (1, 2): 2, (2, 1): 3}
    HW = 2 * D + 1
    YW = D + 1
    NQ = BLOCKS * QUARTERS
    assert TJ * P == BLK and BLOCKS * TJ == JT and QC == 4 and BLOCKS == CHUNKS

    strips, segments, segment_at = [], [], {}

    def add_segment(lo, hi, when):
        if hi > lo:
            segment_at.setdefault(when, []).append(len(segments))
            segments.append((len(strips), lo, hi))

    for s in range(BLOCKS - 1):
        for q in range(QUARTERS):
            when = (s + 1, QUARTERS - 1) if q == 0 else (s + 2, q - 1)
            add_segment(-(-(s + 1) * q // QUARTERS), -(-(s + 1) * (q + 1) // QUARTERS), when)
        strips.append((s, 0, s + 1))
    upper = [BLOCKS - 1]
    while len(upper) < BLOCKS:
        n = len(upper)
        upper.append((n - 1) // 2 if n % 2 else BLOCKS - 1 - n // 2)
    assert sorted(upper) == list(range(BLOCKS))
    for n, s in enumerate(upper):
        first = s + 1 if n else 0
        for lo in range(first, BLOCKS, UP_SEG):
            add_segment(lo, min(lo + UP_SEG, BLOCKS), ("upper", n))
        strips.append((s, first, BLOCKS))
    LOWER = BLOCKS - 1
    UPPER_SEGMENTS = [z for z, (m, _, _) in enumerate(segments) if m >= LOWER]

    def unpacked_upto(z):
        return z + 1 + max(0, z + 1 - UPPER_SEGMENTS[0])

    strip_last_segment = {m: z for z, (m, _, _) in enumerate(segments)}
    units_before, n = [], 0
    for _, lo, hi in segments:
        units_before.append(n)
        n += TJ * (hi - lo)
    units_upto_strip = {m: units_before[z] + TJ * (segments[z][2] - segments[z][1])
                        for m, z in strip_last_segment.items()}

    def prob_half(z, b):
        return (units_before[z] // TJ + b) % 2

    def row_slot(m):
        return (m if m < LOWER else m - LOWER + 1) % 2

    def times_loaded(n):
        return (n + 1) // 2

    gt_dram = nc.dram_tensor("gt_bits", [BLOCKS, P, CHUNKS // 2, BLK], U8, kind="Internal").ap()
    r_dram = nc.dram_tensor("r_rows", [BLOCKS, 1, BLK], F32, kind="Internal").ap()
    x1_dram = nc.dram_tensor("x1_rows", [BLOCKS, P, TJ, D], F32, kind="Internal").ap()
    low_dram = nc.dram_tensor("lower_sums", [BLOCKS, P, TJ, YW], F32, kind="Internal").ap()

    ctx = ExitStack()
    with ctx:
        def sb(name, shape, dt):
            return ctx.enter_context(nc.sbuf_tensor(name, shape, dt))

        def ps(name, shape):
            return ctx.enter_context(nc.psum_tensor(name, shape, F32))

        def sem(name):
            return ctx.enter_context(nc.semaphore(name))

        h = sb("h", [P, JT, HW], F16)
        y = sb("y", [P, JT, YW], F32)
        adj_in = sb("adj_in", [P, ADJ_RING, TJ, BLK], I32)
        eq = sb("eq", [P, EQ_RING, TJ, BLK], BF16)
        gt = sb("gt", [P, GT_RING, TJ, BLK], U8)
        bits_out = sb("bits_out", [P, 2, QC // 2, BLK], U8)
        bits_in = sb("bits_in", [P, 2, SEG // 2 + 1, BLK], U8)
        strip_mask = sb("strip_mask", [P, SEG, TJ, BLK], U8)
        prob = sb("prob", [P, 2, TJ, BLK], F32)
        r_row = sb("r_row", [P, 2, BLK], F32)
        strip_sum = sb("strip_sum", [P, 2, TJ, YW], F32)
        low_in = sb("low_in", [P, 2, TJ, YW], F32)
        xb = sb("xb", [P, TJ, D], F32)
        x1 = sb("x1", [P, 2, TJ, D], F32)
        agg_raw = low_in[:].rearrange("p r t f -> p (r t f)")[:, 0:TJ * HW].rearrange("p (t f) -> p t f", t=TJ)
        agg = sb("agg", [P, TJ, D], F32)
        feat_t = sb("feat_t", [P, TJ, P], F32)
        stats = sb("stats", [P, JT, 6], F32)
        mean_var = sb("mean_var", [P, JT, 2], F32)
        rstd = sb("rstd", [P, JT], F32)
        rdeg = sb("rdeg", [P, TJ], F32)
        g_col = sb("g_col", [P, JT], F32)
        v_col = sb("v_col", [P, TJ], F32)
        fin_rec = sb("fin_rec", [P, 2, TJ], F32)
        ident = sb("ident", [P, P], F32)
        w0t_s = sb("w0t_s", [P, D], F32)
        w1_s = sb("w1_s", [P, D], F32)
        b_s = sb("b_s", [P, D], F32)
        a_s = sb("a_s", [P, 2, D], F32)
        wa = sb("wa", [P, 2], F32)
        wa_rep = sb("wa_rep", [P, 2, P], F32)
        ones = sb("ones", [P, P], F32)
        vmax = sb("vmax", [P, 1], F32)
        cst = sb("cst", [P, 6], F32)
        g_bias, f_bias, r_bias = cst[:, 0:1], cst[:, 1:2], cst[:, 2:3]
        gate_bias, eps, scaled_eps = cst[:, 3:4], cst[:, 4:5], cst[:, 5:6]
        adj_flat = adj_in[:].rearrange("p r t f -> p (r t f)").bitcast(U8)
        MASK_BYTES = UP_SEG * TJ * BLK
        up_mask = adj_flat[:, 0:2 * MASK_BYTES].rearrange("p (r b t f) -> p r b t f", r=2, b=UP_SEG, t=TJ)
        up_bits = adj_flat[:, 2 * MASK_BYTES:2 * MASK_BYTES + 2 * (UP_SEG // 2 + 1) * BLK].rearrange(
            "p (r b f) -> p r b f", r=2, b=UP_SEG // 2 + 1)

        def pairs_of(z):
            _, lo, hi = segments[z]
            return lo // 2, (hi + 1) // 2

        def bits_of(z):
            first, end = pairs_of(z)
            return (bits_in if segments[z][0] < LOWER else up_bits)[:, z % 2, 0:end - first, :]

        def mask_of(z):
            m, lo, hi = segments[z]
            return strip_mask[:, 0:hi - lo] if m < LOWER else up_mask[:, z % 2, 0:hi - lo]

        neg = feat_t
        pos = agg
        junk = agg

        bank = 512
        agg_ps = ps("agg_ps", [P, TJ, bank])
        strip_ps = ps("strip_ps", [P, 2, bank])
        turn_ps = ps("turn_ps", [P, bank])
        proj_ps = ps("proj_ps", [P, bank])

        def strip_banks(m):
            return strip_ps[:] if m < LOWER or (m - LOWER) % 2 == 0 else agg_ps[:, 0:2]

        def strip_out(m, i):
            return strip_banks(m)[:, i // 2, (i % 2) * YW:(i % 2 + 1) * YW]

        const_loaded = sem("const_loaded")
        x_loaded = [sem(f"x_loaded{q}") for q in range(QUARTERS)]
        adj_loaded = [sem(f"adj_loaded{r}") for r in range(ADJ_RING)]
        bits_stored = [sem(f"bits_stored{r}") for r in range(2)]
        bits_loaded = [sem(f"bits_loaded{r}") for r in range(2)]
        xblk_loaded = sem("xblk_loaded")
        rows_stored = [sem(f"rows_stored{r}") for r in range(2)]
        sums_stored = [sem(f"sums_stored{r}") for r in range(2)]
        r_loaded = [sem(f"r_loaded{r}") for r in range(2)]
        rest_loaded = [sem(f"rest_loaded{r}") for r in range(2)]
        out_stored = sem("out_stored")
        ident_zero = sem("ident_zero")
        ident_made = sem("ident_made")
        xb_made = sem("xb_made")
        ln_stat = sem("ln_stat")
        ln_std = sem("ln_std")
        ln_inv = sem("ln_inv")
        ln_made = [sem(f"ln_made{q}") for q in range(QUARTERS)]
        ln_high = sem("ln_high")
        h_made = sem("h_made")
        wa_made = sem("wa_made")
        norm_made = sem("norm_made")
        norm_taken = sem("norm_taken")
        vmax_made = sem("vmax_made")
        dve_step = sem("dve_step")
        pool_step = sem("pool_step")
        eq_made = sem("eq_made")
        gt_made = sem("gt_made")
        pairs_made = sem("pairs_made")
        quads_made = sem("quads_made")
        bits_made = sem("bits_made")
        masks_made = sem("masks_made")
        eq_used = sem("eq_used")
        agg_taken = sem("agg_taken")
        agg_made = sem("agg_made")
        turn_done = sem("turn_done")
        turn_taken = sem("turn_taken")
        proj_done = sem("proj_done")
        x1_made = sem("x1_made")
        dev_ready = sem("dev_ready")
        std_made = sem("std_made")
        h1_made = sem("h1_made")
        v_made = sem("v_made")
        gf_made = sem("gf_made")
        u_made = sem("u_made")
        y_made = sem("y_made")
        r_made = sem("r_made")
        prob_made = sem("prob_made")
        prob_used = sem("prob_used")
        strip_taken = sem("strip_taken")
        rec_made = sem("rec_made")
        neg_made = sem("neg_made")
        exp_made = sem("exp_made")
        out_made = sem("out_made")

        block = ctx.enter_context(nc.Block())

        @block.sync
        def _(sp):
            def load_adj(g):
                if g >= ADJ_RING:
                    sp.wait_ge(eq_made, g - ADJ_RING + 1)
                    sp.wait_ge(gt_made, g - ADJ_RING + 1)
                sp.dma_start(adj_in[:, g % ADJ_RING], adj[g // CHUNKS, g % CHUNKS])\
                  .then_inc(adj_loaded[g % ADJ_RING], 16)

            def store_bits(Q):
                t, q = divmod(Q, QUARTERS)
                sp.wait_ge(bits_made, Q + 1)
                sp.dma_start(gt_dram[t, :, q * QC // 2:(q + 1) * QC // 2, :], bits_out[:, Q % 2])\
                  .then_inc(bits_stored[Q % 2], 16)

            def load_bits(z):
                m, lo, hi = segments[z]
                s = strips[m][0]
                for r in range(2):
                    sp.wait_ge(bits_stored[r], 16 * (s + 1) * QUARTERS // 2)
                if z >= 2:
                    sp.wait_ge(masks_made, unpacked_upto(z - 2))
                if m == LOWER:
                    sp.wait_ge(eq_made, BLOCKS * CHUNKS)
                    sp.wait_ge(gt_made, BLOCKS * CHUNKS)
                first, end = pairs_of(z)
                sp.dma_start(bits_of(z), gt_dram[s, :, first:end, :])\
                  .then_inc(bits_loaded[z % 2], 16)

            def load_x_block(t):
                if t >= 1:
                    sp.wait_ge(x1_made, t)
                sp.dma_start(xb[:], x[t * TJ:(t + 1) * TJ].rearrange("t p d -> p t d")).then_inc(xblk_loaded, 16)

            def store_rows(t):
                sp.wait_ge(x1_made, t + 1)
                sp.dma_start(x1_dram[t], x1[:, t % 2]).then_inc(rows_stored[t % 2], 16)
                sp.wait_ge(r_made, t + 1)
                sp.dma_start(r_dram[t], r_row[0:1, t % 2, :]).then_inc(rows_stored[t % 2], 16)

            def store_sums(s):
                sp.wait_ge(strip_taken, s + 1)
                sp.dma_start(low_dram[s], strip_sum[:, s % 2]).then_inc(sums_stored[s % 2], 16)

            def load_r(n):
                m = LOWER + n
                for r in range(2):
                    sp.wait_ge(rows_stored[r], 32 * BLOCKS // 2)
                sp.wait_ge(prob_made, units_upto_strip[m - 2])
                sp.dma_start(r_row[:, row_slot(m), :], r_dram[upper[n], 0].partition_broadcast(P)).then_inc(r_loaded[row_slot(m)], 16)

            def load_rest(n):
                slot = row_slot(LOWER + n)
                if n >= 2:
                    sp.wait_ge(out_made, n - 1)
                for r in range(2):
                    sp.wait_ge(sums_stored[r], 16 * ((LOWER + 1 - r) // 2))
                sp.dma_start(x1[:, slot], x1_dram[upper[n]]).then_inc(rest_loaded[slot], 16)
                sp.dma_start(low_in[:, slot], low_dram[upper[n]]).then_inc(rest_loaded[slot], 16)

            def store_out(n):
                s = upper[n]
                sp.wait_ge(out_made, n + 1)
                sp.dma_start(out[s * TJ:(s + 1) * TJ].rearrange("t p d -> p t d"), pos[:]).then_inc(out_stored, 16)

            for g in range(ADJ_RING + QC):
                load_adj(g)
            for t in range(BLOCKS + 1):
                for q in range(QUARTERS):
                    Q = t * QUARTERS + q
                    for z in segment_at.get(divmod(Q + 1, QUARTERS), []):
                        load_bits(z)
                    for g in range((Q + 1) * QC + ADJ_RING, (Q + 2) * QC + ADJ_RING):
                        if g < BLOCKS * CHUNKS:
                            load_adj(g)
                    if t < BLOCKS:
                        store_bits(Q)
                    if q == 2 and t < BLOCKS:
                        load_x_block(t)
                    if q == 0 and t >= 2:
                        store_rows(t - 2)
                    if q == 0 and t >= 3:
                        store_sums(t - 3)
            for n in range(BLOCKS):
                if n >= 1:
                    load_r(n)
                for z in segment_at["upper", n]:
                    load_bits(z)
                if n == 0:
                    store_rows(BLOCKS - 1)
                    store_sums(LOWER - 1)
                else:
                    load_rest(n)
                if n >= 2:
                    store_out(n - 2)
            store_out(BLOCKS - 2)
            store_out(BLOCKS - 1)
            sp.wait_ge(out_stored, 16 * BLOCKS)

        @block.gpsimd
        def _(pool):
            nc.gpsimd.memset(ident[:], 0.0).then_inc(ident_zero, 1)
            nc.gpsimd.memset(ones[:], 1.0).then_inc(ident_zero, 1)
            nc.gpsimd.memset(h[:, :, 2 * D:HW], H_SCALE).then_inc(ident_zero, 1)
            nc.gpsimd.memset(cst[:, 2:3], LIFT).then_inc(ident_zero, 1)
            nc.gpsimd.memset(cst[:, 3:4], -GATE / 2).then_inc(ident_zero, 1)
            nc.gpsimd.memset(cst[:, 4:5], LN_EPS).then_inc(ident_zero, 1)
            nc.gpsimd.memset(cst[:, 5:6], LN_EPS / H_SCALE ** 2).then_inc(ident_zero, 1)
            pool.wait_ge(ident_zero, 7)
            nc.gpsimd.affine_select(out=ident[:], in_=ident[:], compare_op=ALU.not_equal, fill=1.0, base=0,
                                    pattern=[[-1, P]], channel_multiplier=1).then_inc(ident_made, 1)
            for q in (1, 3):
                n = JT // QUARTERS
                pool.wait_ge(ln_inv, q // 2 + 1)
                for j in range(q * n, (q + 1) * n):
                    last = nc.gpsimd.tensor_scalar(y[:, j, 0:D], y[:, j, 0:D], mean_var[:, j, 0:1],
                                                   rstd[:, j:j + 1], ALU.subtract, ALU.mult)
                last.then_inc(ln_made[q], 1)
            pool.wait_ge(const_loaded, 16 * 5)
            links = [0]

            def link(instruction):
                links[0] += 1
                instruction.then_inc(pool_step, 1)
                pool.wait_ge(pool_step, links[0])

            for t in range(BLOCKS):
                pool.wait_ge(agg_taken, t + 1)
                if t >= 1:
                    pool.wait_ge(turn_done, 3 * t - 1)
                    pool.wait_ge(v_made, t)
                nc.gpsimd.tensor_tensor(agg[:], agg_raw[:, :, 0:D], agg_raw[:, :, D:2 * D],
                                        ALU.add).then_inc(agg_made, 1)
                pool.wait_ge(xblk_loaded, 16 * (t + 1))
                for i in range(TJ):
                    last = nc.gpsimd.tensor_tensor(xb[:, i, :], xb[:, i, :], b_s[:], ALU.add)
                last.then_inc(xb_made, 1)

            for n in range(BLOCKS):
                slot = row_slot(LOWER + n)
                if n == 0:
                    pool.wait_ge(rows_stored[slot], 32 * BLOCKS // 2)
                else:
                    pool.wait_ge(rest_loaded[slot], 32 * times_loaded(n))
                link(nc.gpsimd.tensor_scalar(x1[:, slot], x1[:, slot], -1.0, None, ALU.add))
                pool.wait_ge(exp_made, n + 1)
                link(nc.gpsimd.tensor_tensor(pos[:], pos[:], x1[:, slot], ALU.add))
                nc.gpsimd.tensor_tensor(pos[:], pos[:], neg[:], ALU.add).then_inc(out_made, 1)

        @block.scalar
        def _(act):
            for q in range(QUARTERS):
                n = JT // QUARTERS
                act.dma_start(y[:, q * n:(q + 1) * n, 0:D],
                              x[q * n:(q + 1) * n].rearrange("t p d -> p t d")).then_inc(x_loaded[q], 16)
            act.dma_start(w1_s[:], w1).then_inc(const_loaded, 16)
            act.dma_start(w0t_s[:], w0t).then_inc(const_loaded, 16)
            act.dma_start(b_s[:], b0.partition_broadcast(P)).then_inc(const_loaded, 16)
            act.dma_start(a_s[:, 0, :], a[0].partition_broadcast(P)).then_inc(const_loaded, 16)
            act.dma_start(a_s[:, 1, :], a[1].partition_broadcast(P)).then_inc(const_loaded, 16)
            act.wait_ge(ident_made, 1)

            def gate(Q, p):
                g = Q * QC + p
                if Q < NQ:
                    act.wait_ge(adj_loaded[g % ADJ_RING], 16 * (g // ADJ_RING + 1))
                    if Q >= 2:
                        act.wait_ge(bits_made, Q - 1)
                    nc.scalar.activation(gt[:, g % GT_RING], adj_in[:, g % ADJ_RING], ACT.Sigmoid,
                                         bias=gate_bias, scale=GATE).then_inc(gt_made, 1)

            def ln_std_of(q):
                n = JT // QUARTERS
                j = slice(q * n, (q + 2) * n)
                act.wait_ge(ln_stat, q + 2)
                nc.scalar.activation(rstd[:, j], mean_var[:, j, 1], ACT.Sqrt, bias=scaled_eps,
                                     scale=H_SCALE ** -2).then_inc(ln_std, 1)

            def high_half(q):
                n = JT // QUARTERS
                j = slice(q * n, (q + 1) * n)
                act.wait_ge(ln_made[q], 1)
                nc.scalar.activation(h[:, j, 0:D], y[:, j, 0:D], ACT.Relu).then_inc(ln_high, 1)

            def take_strip(m):
                act.wait_ge(prob_used, units_upto_strip[m])
                if 2 <= m < LOWER + 2:
                    act.wait_ge(sums_stored[m % 2], 16 * (m // 2))
                if m >= LOWER + 2:
                    act.wait_ge(out_made, m - LOWER - 1)
                for b in range(2):
                    last = nc.scalar.activation(strip_sum[:, m % 2, 2 * b:2 * b + 2, :],
                                                strip_banks(m)[:, b, 0:2 * YW].rearrange("p (t f) -> p t f", t=2),
                                                ACT.Copy)
                last.then_inc(strip_taken, 1)

            def elu_parts(n):
                m = LOWER + n
                act.wait_ge(rec_made, n + 1)
                if n >= 1:
                    act.wait_ge(out_stored, 16 * n)
                for i in range(TJ):
                    last = nc.scalar.activation(neg[:, i, :], strip_sum[:, m % 2, i, 0:D], ACT.Relu,
                                                scale=fin_rec[:, 1, i:i + 1])
                last.then_inc(neg_made, 1)
                for i in range(TJ):
                    nc.scalar.activation(pos[:, i, :], strip_sum[:, m % 2, i, 0:D], ACT.Relu,
                                         scale=fin_rec[:, 0, i:i + 1])
                act.wait_ge(neg_made, n + 1)
                nc.scalar.activation(neg[:], neg[:], ACT.Exp, scale=-1.0).then_inc(exp_made, 1)

            def take_turn(n):
                t, second = divmod(n, 2)
                act.wait_ge(turn_done, 3 * t + second + 1)
                if second == 0 and t >= 1:
                    act.wait_ge(turn_done, 3 * t)
                if second == 1:
                    act.wait_ge(proj_done, 2 * t + 1)
                nc.scalar.activation(feat_t[:].rearrange("p t f -> p (t f)"), turn_ps[:],
                                     ACT.Relu if second else ACT.Copy).then_inc(turn_taken, 1)

            def take_sums(t):
                act.wait_ge(eq_used, CHUNKS * (t + 1))
                if t >= 1:
                    act.wait_ge(agg_made, t)
                    act.wait_ge(x1_made, t)
                nc.scalar.activation(agg_raw, agg_ps[:, :, 0:HW], ACT.Copy).then_inc(agg_taken, 1)

            def std(e):
                act.wait_ge(dev_ready, e + 1)
                nc.scalar.activation(rstd[:, 0:TJ], mean_var[:, 0:TJ, 1], ACT.Sqrt, bias=eps).then_inc(std_made, 1)

            def factors(e):
                if e == 0:
                    act.wait_ge(vmax_made, 2)
                js = slice(e * TJ, (e + 1) * TJ)
                act.wait_ge(v_made, e + 1)
                nc.scalar.activation(g_col[:, js], v_col[:], ACT.Exp, bias=g_bias, scale=1.0 - LEAK)
                nc.scalar.activation(y[:, js, D], v_col[:], ACT.Exp, bias=f_bias, scale=LEAK).then_inc(gf_made, 1)
                act.wait_ge(turn_done, 3 * e + 3)
                if e >= 2:
                    act.wait_ge(rows_stored[e % 2], 32 * (e // 2))
                    act.wait_ge(prob_made, units_upto_strip[e - 2])
                nc.scalar.activation(r_row[:, e % 2, :], turn_ps[:], ACT.Relu, bias=vmax[:, 0:1]).then_inc(u_made, 1)
                act.wait_ge(u_made, e + 1)
                nc.scalar.activation(r_row[:, e % 2, :], r_row[:, e % 2, :], ACT.Exp, bias=r_bias,
                                     scale=LEAK - 1.0).then_inc(r_made, 1)
                act.wait_ge(gf_made, e + 1)
                for i in range(TJ):
                    last = nc.scalar.activation(y[:, e * TJ + i, 0:D], proj_ps[:, i * D:(i + 1) * D],
                                                ACT.Copy, scale=y[:, e * TJ + i, D:YW])
                last.then_inc(y_made, 1)

            ln_std_of(0)
            for p in range(QC):
                gate(0, p)
                if p == 0:
                    high_half(0)
            for t in range(BLOCKS + 1):
                e = t - 1
                for q in range(QUARTERS):
                    Q = t * QUARTERS + q
                    if q == 0 and e >= 0:
                        take_sums(e)
                    if q == QUARTERS - 1 and t >= 2:
                        take_strip(t - 2)
                    if q == 2 and e >= 0:
                        take_turn(2 * e + 1)
                    for p in range(QC):
                        gate(Q + 1, p)
                        if (q, p) == (0, 1) and e >= 0:
                            take_turn(2 * e)
                        if (q, p) == (1, 2) and e >= 0:
                            std(e)
                        if t == 0 and (q, p) == (1, 1):
                            ln_std_of(2)
                        if t == 0 and (q, p) in HIGH_AT:
                            high_half(HIGH_AT[q, p])
                    if q == 2 and e >= 0:
                        factors(e)
                    if q == 3 and t == 0:
                        act.wait_ge(norm_made, 1)
                        nc.scalar.activation(vmax[:], turn_ps[:, 0:1], ACT.Sqrt, scale=float(D))\
                          .then_inc(norm_taken, 1)
            for n in range(BLOCKS):
                if n >= 1:
                    elu_parts(n - 1)
                take_strip(LOWER + n)
            elu_parts(BLOCKS - 1)

        @block.vector
        def _(dve):
            links = [0]

            def link(instruction):
                links[0] += 1
                instruction.then_inc(dve_step, 1)
                dve.wait_ge(dve_step, links[0])

            def statistics(q):
                n = JT // QUARTERS
                dve.wait_ge(x_loaded[q], 16)
                for j in range(q * n, (q + 1) * n):
                    last = nc.vector.bn_stats(stats[:, j, :], y[:, j, 0:D])
                link(last)
                for j in range(q * n, (q + 1) * n):
                    last = nc.vector.bn_aggr(mean_var[:, j, :], stats[:, j, :])
                last.then_inc(ln_stat, 1)

            def invert_std(q):
                js = slice(q * (JT // QUARTERS), (q + 2) * (JT // QUARTERS))
                dve.wait_ge(ln_std, q // 2 + 1)
                nc.vector.reciprocal(rstd[:, js], rstd[:, js]).then_inc(ln_inv, 1)

            def normalize(q):
                n = JT // QUARTERS
                dve.wait_ge(ln_stat, q + 1)
                dve.wait_ge(ln_inv, q // 2 + 1)
                for j in range(q * n, (q + 1) * n):
                    last = nc.vector.tensor_scalar(y[:, j, 0:D], y[:, j, 0:D], mean_var[:, j, 0:1],
                                                   rstd[:, j:j + 1], ALU.subtract, ALU.mult)
                last.then_inc(ln_made[q], 1)

            def low_half(q):
                n = JT // QUARTERS
                js = slice(q * n, (q + 1) * n)
                dve.wait_ge(ln_made[q], 1)
                dve.wait_ge(ln_high, q + 1)
                nc.vector.scalar_tensor_tensor(out=h[:, js, D:2 * D], in0=y[:, js, 0:D], scalar=0.0,
                                               in1=h[:, js, 0:D], op0=ALU.max, op1=ALU.subtract)\
                    .then_inc(h_made, 1)

            def equal(Q, p):
                g = Q * QC + p
                if Q < NQ:
                    dve.wait_ge(adj_loaded[g % ADJ_RING], 16 * (g // ADJ_RING + 1))
                    if g >= EQ_RING:
                        dve.wait_ge(eq_used, g - EQ_RING + 1)
                    nc.vector.tensor_scalar(eq[:, g % EQ_RING], adj_in[:, g % ADJ_RING], 1.0, None,
                                            ALU.is_equal).then_inc(eq_made, 1)

            def pack(Q):
                dve.wait_ge(gt_made, QC * (Q + 1))
                if Q >= 2:
                    dve.wait_ge(bits_stored[Q % 2], 16 * (Q // 2))
                half = slice((Q % 2) * QC, (Q % 2 + 1) * QC)
                g4 = gt[:, half].rearrange("p c (h k) f -> p (c h) k f", k=2).bitcast(I32)
                nc.vector.scalar_tensor_tensor(out=g4[:, :, 0, :], in0=g4[:, :, 0, :], scalar=1, in1=g4[:, :, 1, :],
                                               op0=ALU.logical_shift_left,
                                               op1=ALU.bitwise_or).then_inc(pairs_made, 1)
                dve.wait_ge(pairs_made, Q + 1)
                g2 = gt[:, half].bitcast(I32)
                nc.vector.scalar_tensor_tensor(out=g2[:, :, 0, :], in0=g2[:, :, 0, :], scalar=2,
                                               in1=g2[:, :, 2, :], op0=ALU.logical_shift_left,
                                               op1=ALU.bitwise_or).then_inc(quads_made, 1)
                dve.wait_ge(quads_made, Q + 1)
                nc.vector.scalar_tensor_tensor(out=bits_out[:, Q % 2].bitcast(I32), in0=g2[:, 0::2, 0, :],
                                               scalar=TJ, in1=g2[:, 1::2, 0, :], op0=ALU.logical_shift_left,
                                               op1=ALU.bitwise_or).then_inc(bits_made, 1)

            def unpack(z):
                m, lo, hi = segments[z]
                s = strips[m][0]
                dve.wait_ge(bits_loaded[z % 2], 16 * (z // 2 + 1))
                reused = z - 1 if m < LOWER else z - 2
                if m >= LOWER and reused < UPPER_SEGMENTS[0]:
                    dve.wait_ge(gt_made, BLOCKS * CHUNKS)
                    dve.wait_ge(eq_made, BLOCKS * CHUNKS)
                elif reused >= 0:
                    dve.wait_ge(prob_made, units_before[reused + 1])
                unpack_tiles(z, range(TJ) if m < LOWER else range(TJ // 2))

            def unpack_tiles(z, tiles):
                _, lo, hi = segments[z]
                first_pair = pairs_of(z)[0]
                for k in tiles:
                    for odd in (0, 1):
                        first = lo + (odd - lo) % 2
                        n = len(range(first, hi, 2))
                        if n:
                            pair = first // 2 - first_pair
                            last = nc.vector.tensor_scalar(
                                mask_of(z)[:, first - lo::2, k, :].bitcast(I32),
                                bits_of(z)[:, pair:pair + n, :].bitcast(I32),
                                TJ * (1 - odd) + TJ - 1 - k, 0x01010101, ALU.logical_shift_right, ALU.bitwise_and)
                last.then_inc(masks_made, 1)

            def unpack_rest(z):
                unpack_tiles(z, range(TJ // 2, TJ))

            def weights(z, b, half):
                m, lo, hi = segments[z]
                s = strips[m][0]
                if isinstance(b, int) and b == 0:
                    if m <= LOWER:
                        dve.wait_ge(r_made, s + 1)
                    else:
                        dve.wait_ge(r_loaded[row_slot(m)], 16 * times_loaded(m - LOWER))
                    dve.wait_ge(masks_made, unpacked_upto(z))
                for k in range(TJ):
                    if not isinstance(b, int) or units_before[z] + b * TJ >= 2 * TJ:
                        dve.wait_ge(prob_used, b * TJ + (units_before[z] + k - 2 * TJ + 1))
                    nc.vector.scalar_tensor_tensor(
                        out=prob[:, half, k, :], in0=r_row[:, row_slot(m), :],
                        scalar=g_col[:, bass.ds(b * TJ + (lo * TJ + k), 1)],
                        in1=mask_of(z)[:, bass.ds(b, 1), k, :].rearrange("p o f -> p (o f)"),
                        op0=ALU.max, op1=ALU.mult).then_inc(prob_made, 1)

            def residual_norm(e):
                dve.wait_ge(agg_made, e + 1)
                link(nc.vector.reciprocal(rdeg[:], agg_raw[:, :, 2 * D]))
                dve.wait_ge(proj_done, 2 * e + 1)
                dve.wait_ge(xb_made, e + 1)
                if e >= 2:
                    dve.wait_ge(rows_stored[e % 2], 32 * (e // 2))
                for i in range(TJ):
                    last = nc.vector.scalar_tensor_tensor(out=x1[:, e % 2, i, :], in0=proj_ps[:, i * D:(i + 1) * D],
                                                          scalar=rdeg[:, i:i + 1], in1=xb[:, i, :],
                                                          op0=ALU.mult, op1=ALU.add)
                last.then_inc(x1_made, 1)
                dve.wait_ge(x1_made, e + 1)
                for i in range(TJ):
                    last = nc.vector.bn_stats(stats[:, i, :], x1[:, e % 2, i, :])
                link(last)
                for i in range(TJ):
                    last = nc.vector.bn_aggr(mean_var[:, i, :], stats[:, i, :])
                last.then_inc(dev_ready, 1)

            def second_norm(e):
                dve.wait_ge(dev_ready, e + 1)
                dve.wait_ge(std_made, e + 1)
                link(nc.vector.reciprocal(rstd[:, 0:TJ], rstd[:, 0:TJ]))
                for i in range(TJ):
                    last = nc.vector.tensor_scalar(agg[:, i, :], x1[:, e % 2, i, :], mean_var[:, i, 0:1],
                                                   rstd[:, i:i + 1], ALU.subtract, ALU.mult)
                last.then_inc(h1_made, 1)

            def logits(e):
                dve.wait_ge(proj_done, 2 * e + 2)
                if e >= 1:
                    dve.wait_ge(gf_made, e)
                for i in range(TJ):
                    last = nc.vector.tensor_tensor_reduce(junk[:, i, :], proj_ps[:, i * D:(i + 1) * D], a_s[:, 1, :],
                                                          1.0, 0.0, ALU.mult, ALU.add, v_col[:, i:i + 1])
                last.then_inc(v_made, 1)

            def invert(n):
                m = LOWER + n
                dve.wait_ge(strip_taken, m + 1)
                total = strip_sum[:, m % 2]
                if n >= 1:
                    dve.wait_ge(rest_loaded[row_slot(m)], 32 * times_loaded(n))
                    link(nc.vector.tensor_tensor(total, total, low_in[:, row_slot(m)], ALU.add))
                    dve.wait_ge(exp_made, n)
                link(nc.vector.reciprocal(fin_rec[:, 0, :], total[:, :, D]))
                nc.vector.tensor_scalar(fin_rec[:, 1, :], fin_rec[:, 0, :], -1.0, None,
                                        ALU.mult).then_inc(rec_made, 1)

            statistics(0)
            equal(0, 0)
            statistics(1)
            equal(0, 1)
            invert_std(0)
            normalize(0)
            equal(0, 2)
            low_half(0)
            equal(0, 3)
            for t in range(BLOCKS + 1):
                e = t - 1
                for q in range(QUARTERS):
                    Q = t * QUARTERS + q
                    z = segment_at.get((t, q), [None])[0]
                    blocks = 0 if z is None else segments[z][2] - segments[z][1]
                    for p in range(QC):
                        equal(Q + 1, p)
                        if t == 0:
                            if (q, p) in STATISTICS_AT:
                                statistics(STATISTICS_AT[q, p])
                            if (q, p) == (1, 1):
                                invert_std(2)
                            if (q, p) in NORMALIZE_AT:
                                normalize(NORMALIZE_AT[q, p])
                            if (q, p) in LOW_AT:
                                low_half(LOW_AT[q, p])
                        if e >= 0:
                            if (q, p) == (1, 1):
                                residual_norm(e)
                            if (q, p) == (1, 3):
                                second_norm(e)
                            if (q, p) == (2, 3):
                                logits(e)
                        if p == 0 and blocks:
                            unpack(z)
                        if p == 2 and t < BLOCKS:
                            pack(Q)
                        if p < blocks:
                            weights(z, p, prob_half(z, p))
                    if t == 0 and q == 3:
                        dve.wait_ge(const_loaded, 16 * 5)
                        for k in range(2):
                            link(nc.vector.tensor_tensor_reduce(junk[:, k, :], w1_s[:], a_s[:, k, :], 1.0, 0.0,
                                                                ALU.mult, ALU.add, wa[:, k:k + 1]))
                            last = nc.vector.tensor_scalar(wa_rep[:, k, :], ones[:], wa[:, k:k + 1], None, ALU.mult)
                        last.then_inc(wa_made, 1)
                        dve.wait_ge(norm_taken, 1)
                        nc.vector.tensor_scalar(cst[:, 0:1], vmax[:], LEAK - 1.0, LIFT, ALU.mult,
                                                ALU.add).then_inc(vmax_made, 1)
                        nc.vector.tensor_scalar(cst[:, 1:2], vmax[:], -LEAK, LIFT, ALU.mult,
                                                ALU.add).then_inc(vmax_made, 1)
            unpack(UPPER_SEGMENTS[0])
            unpack_rest(UPPER_SEGMENTS[0])
            for z in UPPER_SEGMENTS:
                m, lo, hi = segments[z]
                s = strips[m][0]
                following = z + 1 if z + 1 < len(segments) else None
                n = hi - lo
                before = m - LOWER - 1 if lo == strips[m][1] and m > LOWER else None
                if n > 1:
                    weights(z, 0, prob_half(z, 0))
                    if before is not None:
                        invert(before)
                pairs = (n - 2) // 2
                if pairs > 1:
                    with dve.Fori(0, pairs) as pair:
                        weights(z, pair * 2 + 1, prob_half(z, 1))
                        weights(z, pair * 2 + 2, prob_half(z, 2))
                for b in range(1 + 2 * pairs if pairs > 1 else 1, n - 1):
                    weights(z, b, prob_half(z, b))
                if following is not None:
                    unpack(following)
                weights(z, n - 1, prob_half(z, n - 1))
                if following is not None:
                    unpack_rest(following)
                if n == 1 and before is not None:
                    invert(before)
            invert(BLOCKS - 1)

        @block.tensor
        def _(pe):
            def aggregate(Q, c, first=False, last=False):
                q = Q % QUARTERS
                pe.wait_ge(eq_made, c + (Q * QC + 1))
                for k in range(TJ):
                    for i in range(TJ):
                        mm = nc.tensor.matmul(
                            agg_ps[:, i, 0:HW],
                            eq[:, bass.ds(c + (Q * QC) % EQ_RING, 1), k,
                               i * P:(i + 1) * P].rearrange("p o f -> p (o f)"),
                            h[:, bass.ds(c * TJ + (q * QC * TJ + k), 1), :].rearrange("p o f -> p (o f)"),
                            start=(first and k == 0), stop=(last and k == TJ - 1))
                mm.then_inc(eq_used, 1)

            def attend(z, b, half, first=False, last=False):
                m, lo, _ = segments[z]
                for k in range(TJ):
                    pe.wait_ge(prob_made, b * TJ + (units_before[z] + k + 1))
                    for i in range(TJ):
                        mm = nc.tensor.matmul(
                            strip_out(m, i), prob[:, half, k, i * P:(i + 1) * P],
                            y[:, bass.ds(b * TJ + (lo * TJ + k), 1), :].rearrange("p o f -> p (o f)"),
                            start=(first and k == 0 and i % 2 == 0), stop=(last and k == TJ - 1),
                            skip_group_check=True)
                    mm.then_inc(prob_used, 1)

            def quarter(Q, z, middle):
                chunks = 0 if Q is None else QC
                blocks = 0 if z is None else segments[z][2] - segments[z][1]
                skip = 0
                ends = {}
                if Q is not None:
                    if Q < QUARTERS:
                        pe.wait_ge(h_made, Q + 1)
                    if Q % QUARTERS == 0:
                        ends.setdefault(0, {})["agg_first"] = True
                        if Q:
                            pe.wait_ge(agg_taken, Q // QUARTERS)
                    if Q % QUARTERS == QUARTERS - 1:
                        ends.setdefault(QC - 1, {})["agg_last"] = True
                        skip = max(0, chunks - blocks)
                if z is not None:
                    m, lo, hi = segments[z]
                    s, first_block, end_block = strips[m]
                    if lo == first_block:
                        ends.setdefault(skip, {})["strip_first"] = True
                    if hi == end_block:
                        ends.setdefault(skip + blocks - 1, {})["strip_last"] = True

                def position(p, half, has_block, end):
                    if chunks:
                        aggregate(Q, p, end.get("agg_first", False), end.get("agg_last", False))
                    if has_block:
                        if "strip_first" in end:
                            if m == LOWER + 1:
                                pe.wait_ge(agg_taken, BLOCKS)
                            elif m >= 1:
                                pe.wait_ge(strip_taken, m if m <= LOWER else m - 1)
                            pe.wait_ge(y_made, s + 1 if m < LOWER else BLOCKS)
                        attend(z, p - skip if skip else p, half, "strip_first" in end, "strip_last" in end)

                p, total = 0, max(chunks, blocks)
                while p < total:
                    if middle and p == total // 2:
                        middle()
                    stop = p + 1
                    while stop < total and not chunks and p not in ends and stop not in ends \
                            and not (middle and stop == total // 2):
                        stop += 1
                    pairs = (stop - p) // 2
                    if pairs > 1:
                        with pe.Fori(0, pairs) as pair:
                            position(pair * 2 + p, prob_half(z, p), True, {})
                            position(pair * 2 + (p + 1), prob_half(z, p + 1), True, {})
                        p += 2 * pairs
                    else:
                        b = p - skip
                        has_block = 0 <= b < blocks
                        position(p, prob_half(z, b) if has_block else None, has_block, ends.get(p, {}))
                        p += 1

            def turn(n):
                e, second = divmod(n, 2)
                pe.wait_ge(h1_made if second else agg_made, e + 1)
                if second:
                    pe.wait_ge(turn_taken, 2 * e + 1)
                elif e >= 1:
                    pe.wait_ge(u_made, e)
                else:
                    pe.wait_ge(norm_taken, 1)
                for i in range(TJ):
                    mm = nc.tensor.transpose(turn_ps[:, i * P:(i + 1) * P], agg[:, i, :], ident[:])
                mm.then_inc(turn_done, 1)

            def project(n):
                e, second = divmod(n, 2)
                pe.wait_ge(turn_taken, n + 1)
                if second:
                    pe.wait_ge(x1_made, e + 1)
                elif e >= 1:
                    pe.wait_ge(y_made, e)
                for i in range(TJ):
                    mm = nc.tensor.matmul(proj_ps[:, i * D:(i + 1) * D], feat_t[:, i, :],
                                          (w1_s if second else w0t_s)[:], start=True, stop=True)
                mm.then_inc(proj_done, 1)

            pe.wait_ge(ident_made, 1)
            for t in range(BLOCKS + 1):
                e = t - 1
                for q in range(QUARTERS):
                    z = segment_at.get((t, q), [None])[0]

                    def turn_first():
                        turn(2 * e)

                    def project_second():
                        project(2 * e + 1)
                        nc.tensor.matmul(turn_ps[:], wa_rep[:, 0, :], feat_t[:].rearrange("p t f -> p (t f)"),
                                         start=True, stop=True).then_inc(turn_done, 1)

                    middle = {0: turn_first, 2: project_second}.get(q) if e >= 0 else None
                    quarter(t * QUARTERS + q if t < BLOCKS else None, z, middle)
                    if q == 0 and e >= 0:
                        project(2 * e)
                    if q == 1 and e >= 0:
                        turn(2 * e + 1)
                    if t == 0 and q == 3:
                        pe.wait_ge(const_loaded, 16 * 5)
                        pe.wait_ge(wa_made, 1)
                        nc.tensor.matmul(turn_ps[:, 0:1], wa_rep[:, 1, :], wa[:, 1:2],
                                         start=True, stop=True).then_inc(norm_made, 1)
            for z in UPPER_SEGMENTS:
                quarter(None, z, None)


def kernel(x, adj, L0_gnn_W, L0_gnn_b, L1_gnn_W, L1_gnn_a):
    import numpy as np
    import concourse.bacc as bacc
    from concourse.bass_utils import run_bass_kernel_spmd

    n, d = x.shape
    blocks, tj, p = 16, 4, 128
    chunks = n // (tj * p)
    blk = n // blocks
    a5 = np.ascontiguousarray(adj.reshape(blocks, blk, chunks, tj, p).transpose(0, 2, 4, 3, 1))
    arrays = {
        "in_x": np.ascontiguousarray(x).reshape(n // p, p, d),
        "in_adj": a5,
        "in_w0t": np.ascontiguousarray(L0_gnn_W.T),
        "in_b0": np.ascontiguousarray(L0_gnn_b),
        "in_w1": np.ascontiguousarray(L1_gnn_W),
        "in_a": np.ascontiguousarray(L1_gnn_a).reshape(2, d),
    }
    nc = bacc.Bacc("TRN2", target_bir_lowering=False, num_devices=1,
                   dynamic_dma_scratch_size=2048)
    args = [nc.dram_tensor(k, v.shape, mybir.dt.from_np(v.dtype), kind="ExternalInput").ap() for k, v in arrays.items()]
    out = nc.dram_tensor("out_rows", (n // p, p, d), F32, kind="ExternalOutput").ap()
    two_layer_gnn(nc, *args, out)
    r = run_bass_kernel_spmd(nc, [arrays], core_ids=[0])
    return r.results[0]["out_rows"].reshape(n, d)
```
